# Optimizing a Trainium2 kernel written in Bass

```python
import numpy as np
import jax
import jax.numpy as jnp

def _softmax(x, axis=-1):
    return jax.nn.softmax(x, axis=axis)

def _gelu(x):
    return jax.nn.gelu(x, approximate=True)

def _silu(x):
    return jax.nn.silu(x)

def _sigmoid(x):
    return jax.nn.sigmoid(x)

def _layernorm(x, axis=-1, eps=1e-05):
    m = jnp.mean(x, axis=axis, keepdims=True)
    v = jnp.var(x, axis=axis, keepdims=True)
    return (x - m) / jnp.sqrt(v + eps)

def _scatter_add(tgt, idx, src, axis=0):
    return tgt.at[idx].add(src)

def _segment_sum(src, seg, n):
    return jax.ops.segment_sum(src, seg, n)
kernel_name = 'mk_adj_preln_d2_adj_r2_99d889'

def setup_inputs(seed: int=0):
    np.random.seed(seed)
    _w = jnp.asarray

    def _rec_inputs():
        import jax
        import jax.numpy as jnp
        _gk = jax.random.key(seed)
        x = -0.0005207 + 1.001 * jax.random.normal(jax.random.fold_in(_gk, 1), (8192, 128), jnp.float32)
        _a = jax.random.bernoulli(jax.random.fold_in(_gk, 2), 0.000976562, (8192, 8192))
        _a = jnp.logical_or(_a, jnp.eye(8192, dtype=bool))
        _af = _a.astype(jnp.float32)
        _af = _af * jax.random.uniform(jax.random.fold_in(_gk, 3), (8192, 8192), jnp.float32, 0.05, 1)
        adj = _af
        return (x, adj)
    x, adj = _rec_inputs()

    def _L0_gnn_setup():
        import jax, jax.numpy as jnp
        import numpy as np
        ALPHA = 0.1
        N, F = (8192, 128)
        key = jax.random.key(seed)
        k1, k2, k3 = jax.random.split(key, 3)
        x = jax.random.normal(k1, (N, F), dtype=jnp.float32)
        adj = jax.random.uniform(k2, (N, N), dtype=jnp.float32)
        h = jax.random.normal(k3, (N, F), dtype=jnp.float32)
        return {'x': x, 'adj': adj, 'h': h}
    _L0_gnn_all = _L0_gnn_setup()
    _L0_gnn_in = {k: v for k, v in _L0_gnn_all.items() if k in ('h',)}
    del _L0_gnn_all

    def _L1_gnn_setup():
        import jax, jax.numpy as jnp
        import numpy as np
        MIN_NORM = 1e-15
        BALL_EPS = 0.004
        C_IN = 1.0
        C_OUT = 1.0

        def _norm(x):
            return jnp.clip(jnp.linalg.norm(x, axis=-1, keepdims=True), MIN_NORM, None)

        def artanh(x):
            return jnp.arctanh(jnp.clip(x, -1.0 + 1e-07, 1.0 - 1e-07))

        def proj(x, c):
            norm = _norm(x)
            maxnorm = (1.0 - BALL_EPS) / jnp.sqrt(c)
            return jnp.where(norm > maxnorm, x / norm * maxnorm, x)

        def expmap0(u, c):
            sc = jnp.sqrt(c)
            un = _norm(u)
            return jnp.tanh(sc * un) * u / (sc * un)

        def logmap0(p, c):
            sc = jnp.sqrt(c)
            pn = _norm(p)
            return artanh(sc * pn) * p / (sc * pn)

        def mobius_add(x, y, c):
            x2 = jnp.sum(x * x, -1, keepdims=True)
            y2 = jnp.sum(y * y, -1, keepdims=True)
            xy = jnp.sum(x * y, -1, keepdims=True)
            num = (1 + 2 * c * xy + c * y2) * x + (1 - c * x2) * y
            denom = 1 + 2 * c * xy + c * c * x2 * y2
            return num / jnp.clip(denom, MIN_NORM, None)

        def mobius_matvec(m, x, c):
            sc = jnp.sqrt(c)
            xn = _norm(x)
            mx = x @ m.T
            mxn = _norm(mx)
            res = jnp.tanh(mxn / xn * artanh(sc * xn)) * mx / (mxn * sc)
            zero_rows = jnp.all(mx == 0, axis=-1, keepdims=True)
            return jnp.where(zero_rows, jnp.zeros_like(res), res)
        key = jax.random.key(seed)
        k1, k2, k3, k4 = jax.random.split(key, 4)
        N, din, dout = (8192, 128, 128)
        x = jax.random.normal(k1, (N, din), dtype=jnp.float32) * 0.01
        adj = jax.random.uniform(k2, (N, N), dtype=jnp.float32)
        adj = adj / jnp.sum(adj, axis=-1, keepdims=True)
        bound = math_bound = float(np.sqrt(2.0) * np.sqrt(6.0 / (din + dout)))
        weight = jax.random.uniform(k3, (dout, din), dtype=jnp.float32, minval=-bound, maxval=bound)
        bias = jax.random.normal(k4, (dout,), dtype=jnp.float32) * 0.01
        return {'x': x, 'adj': adj, 'weight': weight, 'bias': bias}
    _L1_gnn_all = _L1_gnn_setup()
    _L1_gnn_in = {k: v for k, v in _L1_gnn_all.items() if k in ('weight', 'bias')}
    del _L1_gnn_all
    return {'x': x, 'adj': adj, 'L0_gnn_h': _L0_gnn_in['h'], 'L1_gnn_weight': _L1_gnn_in['weight'], 'L1_gnn_bias': _L1_gnn_in['bias']}

def reference(x, adj, L0_gnn_h, L1_gnn_weight, L1_gnn_bias):
    import jax
    import jax.numpy as jnp

    def _L0_gnn_ref(x, adj, h):
        import jax, jax.numpy as jnp
        import numpy as np
        ALPHA = 0.1
        N, F = (8192, 128)
        return (1.0 - ALPHA) * (adj @ x) + ALPHA * h

    def _L1_gnn_ref(x, adj, weight, bias):
        import jax, jax.numpy as jnp
        import numpy as np
        MIN_NORM = 1e-15
        BALL_EPS = 0.004
        C_IN = 1.0
        C_OUT = 1.0

        def _norm(x):
            return jnp.clip(jnp.linalg.norm(x, axis=-1, keepdims=True), MIN_NORM, None)

        def artanh(x):
            return jnp.arctanh(jnp.clip(x, -1.0 + 1e-07, 1.0 - 1e-07))

        def proj(x, c):
            norm = _norm(x)
            maxnorm = (1.0 - BALL_EPS) / jnp.sqrt(c)
            return jnp.where(norm > maxnorm, x / norm * maxnorm, x)

        def expmap0(u, c):
            sc = jnp.sqrt(c)
            un = _norm(u)
            return jnp.tanh(sc * un) * u / (sc * un)

        def logmap0(p, c):
            sc = jnp.sqrt(c)
            pn = _norm(p)
            return artanh(sc * pn) * p / (sc * pn)

        def mobius_add(x, y, c):
            x2 = jnp.sum(x * x, -1, keepdims=True)
            y2 = jnp.sum(y * y, -1, keepdims=True)
            xy = jnp.sum(x * y, -1, keepdims=True)
            num = (1 + 2 * c * xy + c * y2) * x + (1 - c * x2) * y
            denom = 1 + 2 * c * xy + c * c * x2 * y2
            return num / jnp.clip(denom, MIN_NORM, None)

        def mobius_matvec(m, x, c):
            sc = jnp.sqrt(c)
            xn = _norm(x)
            mx = x @ m.T
            mxn = _norm(mx)
            res = jnp.tanh(mxn / xn * artanh(sc * xn)) * mx / (mxn * sc)
            zero_rows = jnp.all(mx == 0, axis=-1, keepdims=True)
            return jnp.where(zero_rows, jnp.zeros_like(res), res)
        mv = mobius_matvec(weight, x, C_IN)
        res = proj(mv, C_IN)
        hyp_bias = proj(expmap0(bias[None, :], C_IN), C_IN)
        h = proj(mobius_add(res, hyp_bias, C_IN), C_IN)
        xt = logmap0(h, C_IN)
        support_t = adj @ xt
        h = proj(expmap0(support_t, C_IN), C_IN)
        xt = jax.nn.relu(logmap0(h, C_IN))
        h = proj(expmap0(xt, C_OUT), C_OUT)
        return h
    h = jnp.maximum(_layernorm(x, axis=-1), 0.0)
    x = x + _L0_gnn_ref(h, adj, L0_gnn_h)
    h = jnp.maximum(_layernorm(x, axis=-1), 0.0)
    x = x + _L1_gnn_ref(h, adj, L1_gnn_weight, L1_gnn_bias)
    return x

_drawn_inputs = setup_inputs


def setup_inputs(seed=0):
    import zlib

    import numpy as np

    out = dict(_drawn_inputs(seed))
    spreads = {}
    factors = {}
    for name, (base, spread) in spreads.items():
        noise = np.random.default_rng([zlib.crc32(name.encode()), seed]).standard_normal(out[name].shape)
        drawn = base * np.exp(spread * noise) if base else spread * noise
        out[name] = jnp.asarray(drawn.astype(out[name].dtype))
    for name, factor in factors.items():
        out[name] = (out[name] * factor).astype(out[name].dtype)
    return out
```

```python
from contextlib import ExitStack

import concourse.bass as bass
import numpy as np
from concourse import mybir
from concourse.alu_op_type import AluOpType as ALU

F32 = mybir.dt.float32
F32R = mybir.dt.float32r
ACT = mybir.ActivationFunctionType
AX = mybir.AxisListType

P = 128
N, F = 8192, 128
CH = 8
BLK = CH * P
NB = N // BLK
HALF = CH // 2
BANK = 512
BANKS = BLK // BANK
PAIR = 2
LOADS = CH // PAIR
SPLITS = 4
ALPHA = 0.1
LN_EPS = 1e-5
MIN_NORM = 1e-15
MAX_NORM = 1.0 - 0.004
ARTANH_MAX = float(np.float32(1.0 - 1e-7))
SERIES_BELOW = 0.25
SERIES = [1.0 / k for k in (13, 11, 9, 7, 5, 3)]


def block_of(i, t):
    return (i + 3 * t + 2) % NB


def build(nc, x, adj, h0, wt, bias, out):
    with ExitStack() as ctx:
        def sb(name, shape, dt=F32):
            return ctx.enter_context(nc.sbuf_tensor(name, shape, dt))

        def sem(name):
            return ctx.enter_context(nc.semaphore(name))

        def psum(name, shape):
            return ctx.enter_context(nc.psum_tensor(name, shape, F32))

        x1_dram = nc.dram_tensor("x1_scratch", (NB, P, CH * F), F32, kind="Internal").ap()

        h = sb("h", [P, NB * CH * F])
        tan = sb("tan", [P, NB * CH * F])
        part = sb("part", [P, NB * BLK])
        raw = sb("raw", [P, CH, BLK])
        a_hi = sb("a_hi", [P, SPLITS, BLK], F32R)
        a_lo = sb("a_lo", [P, SPLITS, BLK], F32R)
        hw_hi = sb("hw_hi", [P, 2, HALF * F], F32R)
        hw_lo = sb("hw_lo", [P, 2, HALF * F], F32R)
        tw_hi = sb("tw_hi", [P, 2, HALF * F], F32R)
        tw_lo = sb("tw_lo", [P, 2, HALF * F], F32R)
        accT = sb("accT", [P, BLK])
        xin = sb("xin", [P, CH, F])
        h0in = sb("h0in", [P, CH, F])
        z = sb("z", [P, CH, F])
        v = sb("v", [P, CH, F])
        sq = sb("sq", [P, CH, F])
        ident = sb("ident", [P, P])
        zeros = sb("zeros", [P, P], mybir.dt.bfloat16)
        zmove = sb("zmove", [P, BANK], mybir.dt.bfloat16)
        w_sb = sb("w_sb", [P, F])
        hb = sb("hb", [P, 1, F])
        y2 = sb("y2", [P, 1])
        bstat = sb("bstat", [P, CH, 6])
        mv = sb("mv", [P, CH, 2])

        def small(name):
            return sb(name, [P, CH])

        c_half, c_mhalf, c_minus, c_eps = (small(n) for n in ("c_half", "c_mhalf", "c_minus", "c_eps"))
        rstd, s_x, s_m, s_d, s_v = small("rstd"), small("s_x"), small("s_m"), small("s_d"), small("s_v")
        s_n, s_r = small("s_n"), small("s_r")
        lnp, lnm, tnh = small("lnp"), small("lnm"), small("tnh")
        arg, co_a, co_b, co_c = small("arg"), small("co_a"), small("co_b"), small("co_c")
        T = [small(f"tmp{n}") for n in range(12)]

        hacc = psum("hacc", [P, BLK])
        tacc = psum("tacc", [P, BLK])
        pt = psum("pt", [P, CH, F])

        const_in = sem("const_in")
        x_in = sem("x_in")
        adj_in = [sem(f"adj_in{q}") for q in range(LOADS)]
        rows_in = sem("rows_in")
        x1_in = sem("x1_in")
        x1_out = sem("x1_out")
        out_out = sem("out_out")
        hi_ready = sem("hi_ready")
        lo_ready = sem("lo_ready")
        chunk_used = sem("chunk_used")
        whi_ready = sem("whi_ready")
        wlo_ready = sem("wlo_ready")
        h_ready = sem("h_ready")
        acc_saved = sem("acc_saved")
        y_psum = sem("y_psum")
        x1_ready = sem("x1_ready")
        h2_ready = sem("h2_ready")
        xn_ready = sem("xn_ready")
        h2t_psum = sem("h2t_psum")
        h2t_ready = sem("h2t_ready")
        mx_psum = sem("mx_psum")
        mx_ready = sem("mx_ready")
        ln1_arg = sem("ln1_arg")
        ln1_ready = sem("ln1_ready")
        mx_sums = sem("mx_sums")
        tanh_arg = sem("tanh_arg")
        tanh_ready = sem("tanh_ready")
        ab_ready = sem("ab_ready")
        v_sum = sem("v_sum")
        ln2_arg = sem("ln2_arg")
        ln2_ready = sem("ln2_ready")
        c_ready = sem("c_ready")
        tan_ready = sem("tan_ready")
        stats_ready = sem("stats_ready")
        rstd_ready = sem("rstd_ready")
        s_psum = sem("s_psum")
        s_ready = sem("s_ready")
        s_sums = sem("s_sums")
        f_arg1, f_tanh1 = sem("f_arg1"), sem("f_tanh1")
        f_arg2, f_ln = sem("f_arg2"), sem("f_ln")
        f_arg3, f_tanh2 = sem("f_arg3"), sem("f_tanh2")
        f_coef = sem("f_coef")
        out_ready = sem("out_ready")
        carried = sem("carried")
        pool_const = sem("pool_const")
        zero_ready = sem("zero_ready")
        b_sum, b_arg, b_tanh, b_coef, b_ready = (sem(f"bias_{n}") for n in ("sum", "arg", "tanh", "coef", "ready"))

        def wait_apart(eng, s, value):
            eng.wait_ge(s, value)
            if not isinstance(value, int):
                eng.sem_inc(carried)

        step_sems = {}

        def steps(eng, name):
            if name not in step_sems:
                step_sems[name] = sem("steps_" + name)
            s, n = step_sems[name], [0]
            eng.sem_clear(s)

            def step(ins):
                n[0] += 1
                ins.then_inc(s, 1)
                eng.wait_ge(s, n[0])

            return step

        def blk(i):
            return bass.ds(i * BLK, BLK)

        def half_blk(j, half):
            return bass.ds(j * BLK + half * (HALF * F), HALF * F)

        def flat(t3):
            return t3[:, :, :].rearrange("p c f -> p (c f)")

        def per_row(s):
            return s[:, :].rearrange("p (c o) -> p c o", o=1).to_broadcast([P, CH, F])

        for_rows = (1, NB)

        def p2_row(k):
            return NB - 1 - k

        def p2_block(k, t):
            return nc.s_assert_within(NB - 1 - k + t, 1, NB - 1,
                                      skip_runtime_bounds_check_because="step k has blocks t <= k only")

        def p2_tasks(k):
            return NB * NB + NB + (k * (k + 1)) // 2

        def finished_row(n):
            return (NB + 1 - n) % NB

        block = ctx.enter_context(nc.Block())

        @block.sync
        def _(sp):
            def load_block(i, j, task, waits=True):
                for q in range(LOADS):
                    if waits:
                        wait_apart(sp, lo_ready, (task - 1) * CH + (q + 1) * PAIR)
                    sp.dma_start(raw[:, q * PAIR:(q + 1) * PAIR, :].rearrange("p c n -> p (c n)"),
                                 adj[i, j, q]).then_inc(adj_in[q], 16)

            def load_rows(n):
                b = n - 1
                sp.dma_start(flat(xin), x[b]).then_inc(rows_in, 16)
                sp.dma_start(flat(h0in), h0[b]).then_inc(rows_in, 16)

            def store_x1(n):
                b = n - 1
                sp.wait_ge(x1_ready, n)
                sp.dma_start(x1_dram[b], flat(xin)).then_inc(x1_out, 16)

            sp.dma_start(w_sb[:, :], wt).then_inc(const_in, 16)
            sp.dma_start(hb[:, 0, :], bias.to_broadcast([P, F])).then_inc(const_in, 16)
            b = block_of(0, 0)
            sp.dma_start(h[:, b * BLK:(b + 1) * BLK], x[b]).then_inc(x_in, 16)
            load_block(0, b, 0, waits=False)
            with sp.Fori(1, NB) as t:
                b = sp.snap((3 * t + 2) % NB)
                sp.wait_ge(x_in, 16 * t)
                sp.dma_start(h[:, blk(b)], x[b]).then_inc(x_in, 16)
                load_block(0, b, t)

            with sp.Fori(*for_rows) as i:
                load_rows(i)
                for t in range(NB):
                    load_block(i, block_of(i, t), i * NB + t)
                    if t == 3:
                        store_x1(i)
                wait_apart(sp, x1_out, 16 * i)

            load_rows(NB)
            for t in range(NB):
                load_block(0, t, NB * NB + t)
                if t == 3:
                    store_x1(NB)
            sp.wait_ge(x1_out, 16 * NB)

            def final_rows(n):
                sp.dma_start(flat(xin), x1_dram[finished_row(n)]).then_inc(x1_in, 16)

            def store_out(n):
                sp.wait_ge(out_ready, n)
                sp.dma_start(out[finished_row(n)], flat(xin)).then_inc(out_out, 16)
                wait_apart(sp, out_out, 16 * n)

            with sp.Fori(0, NB - 1) as k:
                final_rows(k + 1)
                for t in range(NB - 1):
                    with sp.If(k >= t):
                        load_block(p2_row(k), p2_block(k, t), p2_tasks(k) + t)
                store_out(k + 1)
            final_rows(NB)
            store_out(NB)

        @block.scalar
        def _(act):
            def stage(i, j, task, half, use_h, use_t):
                last = None
                if use_h:
                    last = act.activation(hw_hi[:, half, :], h[:, half_blk(j, half)], ACT.Copy)
                if use_t:
                    last = act.activation(tw_hi[:, half, :], tan[:, half_blk(j, half)], ACT.Copy)
                last.then_inc(whi_ready, 1)

            def chunks(task, half, first=False):
                for c in range(half * HALF, (half + 1) * HALF):
                    if c % PAIR == 0:
                        act.wait_ge(adj_in[c // PAIR], (task + 1) * 16)
                    if not first or c >= SPLITS:
                        act.wait_ge(chunk_used, task * CH + c - SPLITS + 1)
                    act.activation(a_hi[:, c % SPLITS, :], raw[:, c, :], ACT.Copy).then_inc(hi_ready, 1)

            def save_acc(n, with_h, with_t, seed_rows=NB):
                last = None
                if with_h:
                    last = act.activation(accT[:, 0:BANK], hacc[:, 0:BANK], ACT.Copy, scale=1.0 - ALPHA)
                if with_t:
                    last = act.activation(with_t, tacc[:, 0:BANK], ACT.Copy)
                last.then_inc(acc_saved, 1)

            def ln_pair(n, arg_sem, done_sem, s):
                act.wait_ge(arg_sem, n)
                act.activation(lnp[:, :], s[:, :], ACT.Ln, bias=1.0, scale=1.0)
                act.activation(lnm[:, :], s[:, :], ACT.Ln, bias=1.0, scale=-1.0).then_inc(done_sem, 1)

            def mid(n, at):
                if at == 5:
                    act.wait_ge(h2t_psum, n)
                    act.activation(accT[:, :], flat(pt), ACT.Copy).then_inc(h2t_ready, 1)
                if at == 7:
                    act.wait_ge(mx_psum, n)
                    act.activation(flat(v), flat(pt), ACT.Copy).then_inc(mx_ready, 1)
                    ln_pair(n, ln1_arg, ln1_ready, arg)
                if at == 10:
                    act.wait_ge(tanh_arg, n)
                    act.activation(tnh[:, :], arg[:, :], ACT.Tanh).then_inc(tanh_ready, 1)
                if at == 12:
                    ln_pair(n, ln2_arg, ln2_ready, arg)

            def final(n, at):
                if at == 2:
                    act.wait_ge(s_psum, n)
                    act.activation(flat(v), flat(pt), ACT.Copy).then_inc(s_ready, 1)
                if at == 4:
                    act.wait_ge(f_arg1, n)
                    act.activation(tnh[:, :], arg[:, :], ACT.Tanh).then_inc(f_tanh1, 1)
                if at == 6:
                    ln_pair(n, f_arg2, f_ln, arg)
                if at == 8:
                    act.wait_ge(f_arg3, n)
                    act.activation(tnh[:, :], arg[:, :], ACT.Tanh).then_inc(f_tanh2, 1)

            act.wait_ge(b_arg, 1)
            act.activation(tnh[:, 0:1], arg[:, 0:1], ACT.Tanh).then_inc(b_tanh, 1)

            def first_row(t, first):
                for half in range(2):
                    if half == 0:
                        act.wait_ge(h_ready, t + 1)
                    stage(0, block_of(0, t), t, half, True, False)
                    chunks(t, half, first)
            first_row(0, True)
            with act.Fori(1, NB) as t:
                first_row(t, False)
            act.wait_ge(chunk_used, NB * CH)
            save_acc(1, True, None)

            with act.Fori(*for_rows) as i:
                for t in range(NB):
                    j, task = act.snap(block_of(i, t)), i * NB + t

                    def halves(use_t):
                        for half in range(2):
                            if use_t and half == 0:
                                act.wait_ge(tan_ready, i if t == NB - 1 else j + 1)
                            stage(i, j, task, half, True, use_t)
                            chunks(task, half)
                            mid(i, 2 * t + half + 1)
                    if t == NB - 1:
                        halves(True)
                    else:
                        with act.If(j < i):
                            halves(True)
                        with act.Else():
                            halves(False)
                act.wait_ge(chunk_used, (i + 1) * NB * CH)
                save_acc(i + 1, True, part[:, bass.ds(i * BLK, BANK)])

            for t in range(NB):
                for half in range(2):
                    if half == 0:
                        act.wait_ge(tan_ready, NB if t == NB - 1 else NB - 1)
                    stage(0, t, NB * NB + t, half, False, True)
                    chunks(NB * NB + t, half)
                    mid(NB, 2 * t + half + 1)
            act.wait_ge(chunk_used, (NB + 1) * NB * CH)
            save_acc(NB + 1, False, accT[:, 0:BANK])

            with act.Fori(0, NB - 1) as k:
                for t in range(NB - 1):
                    task = p2_tasks(k) + t
                    with act.If(k >= t):
                        for half in range(2):
                            stage(p2_row(k), p2_block(k, t), task, half, False, True)
                            chunks(task, half)
                            final(k + 1, 2 * t + half + 1)
                    with act.Else():
                        for half in range(2):
                            final(k + 1, 2 * t + half + 1)
                act.wait_ge(chunk_used, p2_tasks(k + 1) * CH)
                save_acc(NB + 2 + k, False, accT[:, 0:BANK])
            for at in range(9):
                final(NB, at)

        @block.vector
        def _(dve):
            def chunks(task, half):
                for c in range(half * HALF, (half + 1) * HALF):
                    dve.wait_ge(hi_ready, task * CH + c + 1)
                    dve.tensor_tensor(a_lo[:, c % SPLITS, :], raw[:, c, :],
                                      a_hi[:, c % SPLITS, :].bitcast(F32), ALU.subtract).then_inc(lo_ready, 1)

            def save_acc(with_h, with_t):
                last = None
                if with_h:
                    last = dve.tensor_scalar(accT[:, BANK:BLK], hacc[:, BANK:BLK], 1.0 - ALPHA, None, ALU.mult)
                if with_t:
                    last = dve.tensor_copy(with_t, tacc[:, BANK:BLK])
                last.then_inc(acc_saved, 1)

            def stats(src, n, signal, step):
                last = None
                for c in range(CH):
                    last = dve.bn_stats(bstat[:, c, :], src[:, c, :])
                step(last)
                for c in range(CH):
                    last = dve.bn_aggr(mv[:, c, :], bstat[:, c, :])
                last.then_inc(stats_ready, 1)

            def normalise(dst, src, n, step, signal):
                dve.wait_ge(rstd_ready, n)
                last = None
                for c in range(CH):
                    last = dve.tensor_scalar(dst[:, c, :], src[:, c, :], mv[:, c, 0:1], rstd[:, c:c + 1],
                                             ALU.subtract, ALU.mult)
                step(last)
                dve.tensor_scalar(dst[:, :, :], dst[:, :, :], 0.0, None, ALU.max).then_inc(signal, 1)

            def row_sums(dst, src):
                return dve.tensor_reduce(dst[:, :], src[:, :, :], AX.X, ALU.add)

            def norm_h(t):
                step = steps(dve, "norm_h")
                dve.wait_ge(x_in, 16 * (t + 1))
                j = dve.snap((3 * t + 2) % NB) if not isinstance(t, int) else block_of(0, t)
                hj = h[:, blk(j)].rearrange("p (c f) -> p c f", c=CH)
                stats(hj, None, None, step)
                normalise(hj, hj, t + 1, step, h_ready)

            def mid(n, at):
                m = n - 1
                if at == 1:
                    step = steps(dve, "pre")
                    dve.wait_ge(rows_in, 32 * n)
                    step(dve.scalar_tensor_tensor(xin[:, :, :], h0in[:, :, :], ALPHA, xin[:, :, :],
                                                  ALU.mult, ALU.add))
                if at == 3:
                    step = steps(dve, "stats")
                    dve.wait_ge(y_psum, n)
                    dve.tensor_tensor(xin[:, :, :], pt[:, :, :], xin[:, :, :], ALU.add).then_inc(x1_ready, 1)
                    dve.wait_ge(x1_ready, n)
                    stats(xin, None, None, step)
                if at == 4:
                    step = steps(dve, "norm2")
                    normalise(z, xin, NB + n, step, h2_ready)
                if at == 5:
                    step = steps(dve, "xn")
                    dve.wait_ge(h2_ready, n)
                    step(dve.tensor_tensor(sq[:, :, :], z[:, :, :], z[:, :, :], ALU.mult))
                    row_sums(s_x, sq).then_inc(xn_ready, 1)
                if at == 9:
                    step = steps(dve, "mx")
                    dve.wait_ge(mx_ready, n)
                    step(dve.tensor_tensor(sq[:, :, :], v[:, :, :], v[:, :, :], ALU.mult))
                    step(row_sums(s_m, sq))
                    step(dve.tensor_tensor(sq[:, :, :], v[:, :, :], hb[:, :, :].to_broadcast([P, CH, F]), ALU.mult))
                    row_sums(s_d, sq).then_inc(mx_sums, 1)
                if at == 12:
                    step = steps(dve, "v")
                    dve.wait_ge(ab_ready, n)
                    step(dve.tensor_tensor(v[:, :, :], v[:, :, :], per_row(co_a), ALU.mult))
                    step(dve.tensor_tensor(sq[:, :, :], hb[:, :, :].to_broadcast([P, CH, F]), per_row(co_b), ALU.mult))
                    step(dve.tensor_tensor(v[:, :, :], v[:, :, :], sq[:, :, :], ALU.add))
                    step(dve.tensor_tensor(sq[:, :, :], v[:, :, :], v[:, :, :], ALU.mult))
                    row_sums(s_v, sq).then_inc(v_sum, 1)
                if at == 14:
                    dve.wait_ge(c_ready, n)
                    tj = tan[:, blk(m)].rearrange("p (c f) -> p c f", c=CH)
                    dve.tensor_tensor(tj, v[:, :, :], per_row(co_c), ALU.mult).then_inc(tan_ready, 1)

            def final(n, at):
                m = n - 1
                if at == 3:
                    step = steps(dve, "final_sums")
                    dve.wait_ge(s_ready, n)
                    step(dve.tensor_tensor(sq[:, :, :], v[:, :, :], v[:, :, :], ALU.mult))
                    step(row_sums(s_n, sq))
                    step(dve.tensor_scalar(v[:, :, :], v[:, :, :], 0.0, None, ALU.max))
                    step(dve.tensor_tensor(sq[:, :, :], v[:, :, :], v[:, :, :], ALU.mult))
                    row_sums(s_r, sq).then_inc(s_sums, 1)
                if at == 10:
                    step = steps(dve, "final_out")
                    dve.wait_ge(f_coef, n)
                    step(dve.tensor_tensor(v[:, :, :], v[:, :, :], per_row(co_c), ALU.mult))
                    dve.wait_ge(x1_in, 16 * n)
                    dve.tensor_tensor(xin[:, :, :], xin[:, :, :], v[:, :, :], ALU.add).then_inc(out_ready, 1)

            step = steps(dve, "bias")
            dve.wait_ge(const_in, 32)
            step(dve.tensor_tensor(sq[:, 0, :], hb[:, 0, :], hb[:, 0, :], ALU.mult))
            dve.tensor_reduce(s_n[:, 0:1], sq[:, 0, :], AX.X, ALU.add).then_inc(b_sum, 1)
            dve.wait_ge(b_coef, 1)
            step(dve.tensor_scalar(hb[:, 0, :], hb[:, 0, :], co_c[:, 0:1], None, ALU.mult))
            step(dve.tensor_tensor(sq[:, 0, :], hb[:, 0, :], hb[:, 0, :], ALU.mult))
            dve.tensor_reduce(y2[:, 0:1], sq[:, 0, :], AX.X, ALU.add).then_inc(b_ready, 1)

            def first_row(t, norm):
                for half in range(2):
                    chunks(t, half)
                    if norm and half == 0:
                        norm_h(t + 1)
            norm_h(0)
            with dve.Fori(0, NB - 1) as t:
                first_row(t, True)
            first_row(NB - 1, False)
            dve.wait_ge(chunk_used, NB * CH)
            save_acc(True, None)

            with dve.Fori(*for_rows) as i:
                for t in range(NB):
                    for half in range(2):
                        chunks(i * NB + t, half)
                        mid(i, 2 * t + half + 1)
                dve.wait_ge(chunk_used, (i + 1) * NB * CH)
                save_acc(True, part[:, bass.ds(i * BLK + BANK, BANK)])

            for t in range(NB):
                for half in range(2):
                    chunks(NB * NB + t, half)
                    mid(NB, 2 * t + half + 1)
            dve.wait_ge(chunk_used, (NB + 1) * NB * CH)
            save_acc(False, accT[:, BANK:BLK])

            with dve.Fori(0, NB - 1) as k:
                for t in range(NB - 1):
                    task = p2_tasks(k) + t
                    with dve.If(k >= t):
                        for half in range(2):
                            chunks(task, half)
                            final(k + 1, 2 * t + half + 1)
                    with dve.Else():
                        for half in range(2):
                            final(k + 1, 2 * t + half + 1)
                dve.wait_ge(chunk_used, p2_tasks(k + 1) * CH)
                save_acc(False, accT[:, BANK:BLK])
            for at in range(11):
                final(NB, at)

        @block.gpsimd
        def _(pool):
            def stage(j, task, half, use_h, use_t):
                wait_apart(pool, whi_ready, task * 2 + half + 1)
                last = None
                if use_h:
                    last = pool.tensor_tensor(hw_lo[:, half, :], h[:, half_blk(j, half)],
                                              hw_hi[:, half, :].bitcast(F32), ALU.subtract)
                if use_t:
                    last = pool.tensor_tensor(tw_lo[:, half, :], tan[:, half_blk(j, half)],
                                              tw_hi[:, half, :].bitcast(F32), ALU.subtract)
                last.then_inc(wlo_ready, 1)

            def math(step, w):
                def A(t):
                    return t[:, 0:w]

                def tt(o, a, b, op):
                    step(pool.tensor_tensor(A(o), A(a), A(b), op))
                    return o

                def ts(o, a, s1, op1, s2=None, op2=None):
                    if op2 is None:
                        step(pool.tensor_scalar(A(o), A(a), s1, None, op1))
                    else:
                        step(pool.tensor_scalar(A(o), A(a), s1, s2, op1, op2))
                    return o

                def mul(o, a, b):
                    return tt(o, a, b, ALU.mult)

                def root(o, a):
                    return tt(o, a, c_half, ALU.pow)

                def inverse(o, a):
                    return tt(o, a, c_minus, ALU.pow)

                def clip(o, a):
                    return ts(o, a, MIN_NORM, ALU.max)

                def shrink(o, a, t):
                    clip(t, a)
                    inverse(t, t)
                    return ts(o, t, MAX_NORM, ALU.mult, 1.0, ALU.min)

                return tt, ts, mul, root, inverse, clip, shrink

            def artanh(step, o, a, t):
                tt, ts, mul, *_ = math(step, CH)
                a2, s, m = t
                mul(a2, a, a)
                ts(s, a2, SERIES[0], ALU.mult, SERIES[1], ALU.add)
                for k in SERIES[2:]:
                    mul(s, s, a2)
                    ts(s, s, k, ALU.add)
                mul(s, s, a2)
                ts(s, s, 1.0, ALU.add)
                mul(s, s, a)
                tt(o, lnp, lnm, ALU.subtract)
                ts(o, o, 0.5, ALU.mult)
                ts(m, a, SERIES_BELOW, ALU.is_lt)
                tt(s, s, o, ALU.subtract)
                mul(s, s, m)
                return tt(o, o, s, ALU.add)

            def inverse_std(n):
                step = steps(pool, "inverse_std")
                pool.wait_ge(stats_ready, n)
                step(pool.tensor_tensor(rstd[:, :], mv[:, :, 1], c_eps[:, :], ALU.add))
                pool.tensor_tensor(rstd[:, :], rstd[:, :], c_mhalf[:, :], ALU.pow).then_inc(rstd_ready, 1)

            xn, xinv, mraw, minv, scale_, t5, t6, t7, at_, nraw, pn, extra = T

            def mid(n, at):
                m = n - 1
                if at == 3:
                    inverse_std(NB + n)
                if at == 6:
                    step = steps(pool, "m1")
                    tt, ts, mul, root, inverse, clip, shrink = math(step, CH)
                    pool.wait_ge(xn_ready, n)
                    root(xn, s_x)
                    clip(xn, xn)
                    inverse(xinv, xn)
                    pool.tensor_scalar(arg[:, :], xn[:, :], ARTANH_MAX, None, ALU.min).then_inc(ln1_arg, 1)
                if at == 8:
                    step = steps(pool, "m2")
                    tt, ts, mul, root, inverse, clip, shrink = math(step, CH)
                    pool.wait_ge(ln1_ready, n)
                    artanh(step, at_, arg, (t5, t6, t7))
                    mul(at_, at_, xinv)
                if at == 9:
                    step = steps(pool, "m3")
                    tt, ts, mul, root, inverse, clip, shrink = math(step, CH)
                    pool.wait_ge(mx_sums, n)
                    root(mraw, s_m)
                    clip(minv, mraw)
                    mul(t5, at_, minv)
                    inverse(minv, minv)
                    pool.tensor_scalar(arg[:, :], t5[:, :], 1.0, None, ALU.mult).then_inc(tanh_arg, 1)
                if at == 10:
                    step = steps(pool, "m4")
                    tt, ts, mul, root, inverse, clip, shrink = math(step, CH)
                    pool.wait_ge(tanh_ready, n)
                    r, xy, x2, den = t5, t6, t7, xinv
                    mul(r, tnh, minv)
                    mul(nraw, r, mraw)
                    shrink(pn, nraw, extra)
                    mul(r, r, pn)
                    mul(xy, r, s_d)
                    ts(xy, xy, 2.0, ALU.mult, 1.0, ALU.add)
                    mul(x2, r, r)
                    mul(x2, x2, s_m)
                    step(pool.tensor_scalar(den[:, :], x2[:, :], y2[:, 0:1], None, ALU.mult))
                    tt(den, den, xy, ALU.add)
                    clip(den, den)
                    inverse(den, den)
                    step(pool.tensor_scalar(xy[:, :], xy[:, :], y2[:, 0:1], None, ALU.add))
                    mul(xy, xy, r)
                    mul(co_a, xy, den)
                    ts(x2, x2, -1.0, ALU.mult, 1.0, ALU.add)
                    pool.tensor_tensor(co_b[:, :], x2[:, :], den[:, :], ALU.mult).then_inc(ab_ready, 1)
                if at == 12:
                    step = steps(pool, "m5")
                    tt, ts, mul, root, inverse, clip, shrink = math(step, CH)
                    pool.wait_ge(v_sum, n)
                    root(nraw, s_v)
                    shrink(scale_, nraw, extra)
                    mul(pn, nraw, scale_)
                    clip(pn, pn)
                    pool.tensor_scalar(arg[:, :], pn[:, :], ARTANH_MAX, None, ALU.min).then_inc(ln2_arg, 1)
                if at == 13:
                    step = steps(pool, "m6")
                    tt, ts, mul, root, inverse, clip, shrink = math(step, CH)
                    inverse(pn, pn)
                    mul(scale_, scale_, pn)
                    pool.wait_ge(ln2_ready, n)
                    artanh(step, at_, arg, (t5, t6, t7))
                    pool.tensor_tensor(co_c[:, :], at_[:, :], scale_[:, :], ALU.mult).then_inc(c_ready, 1)

            def final(n, at):
                m = n - 1
                if at == 4:
                    step = steps(pool, "f1")
                    tt, ts, mul, root, inverse, clip, shrink = math(step, CH)
                    pool.wait_ge(s_sums, n)
                    root(nraw, s_n)
                    clip(xn, nraw)
                    pool.tensor_scalar(arg[:, :], xn[:, :], 1.0, None, ALU.mult).then_inc(f_arg1, 1)
                    inverse(xinv, xn)
                if at == 5:
                    step = steps(pool, "f2")
                    tt, ts, mul, root, inverse, clip, shrink = math(step, CH)
                    pool.wait_ge(f_tanh1, n)
                    mul(co_a, tnh, xinv)
                    mul(nraw, co_a, nraw)
                    shrink(scale_, nraw, extra)
                    mul(co_a, co_a, scale_)
                    mul(pn, nraw, scale_)
                    clip(pn, pn)
                    pool.tensor_scalar(arg[:, :], pn[:, :], ARTANH_MAX, None, ALU.min).then_inc(f_arg2, 1)
                if at == 7:
                    step = steps(pool, "f3")
                    tt, ts, mul, root, inverse, clip, shrink = math(step, CH)
                    inverse(pn, pn)
                    mul(co_a, co_a, pn)
                    pool.wait_ge(f_ln, n)
                    artanh(step, at_, arg, (t5, t6, t7))
                    mul(co_a, co_a, at_)
                    root(mraw, s_r)
                    mul(mraw, mraw, co_a)
                    clip(minv, mraw)
                    pool.tensor_scalar(arg[:, :], minv[:, :], 1.0, None, ALU.mult).then_inc(f_arg3, 1)
                if at == 9:
                    step = steps(pool, "f4")
                    tt, ts, mul, root, inverse, clip, shrink = math(step, CH)
                    inverse(minv, minv)
                    pool.wait_ge(f_tanh2, n)
                    mul(co_b, tnh, minv)
                    mul(mraw, mraw, co_b)
                    shrink(scale_, mraw, extra)
                    mul(co_b, co_b, scale_)
                    pool.tensor_tensor(co_c[:, :], co_a[:, :], co_b[:, :], ALU.mult).then_inc(f_coef, 1)

            step = steps(pool, "const")
            step(pool.memset(c_half[:, :], 0.5))
            step(pool.memset(c_mhalf[:, :], -0.5))
            step(pool.memset(c_minus[:, :], -1.0))
            step(pool.memset(c_eps[:, :], LN_EPS))
            pool.memset(zeros[:, :], 0.0).then_inc(zero_ready, 1)
            pool.memset(zmove[:, :], 0.0).then_inc(zero_ready, 1)
            step(pool.memset(ident[:, :], 0.0))
            pool.affine_select(out=ident[:, :], in_=ident[:, :], compare_op=ALU.not_equal, fill=1.0,
                               base=0, pattern=[[-1, P]], channel_multiplier=1).then_inc(pool_const, 1)
            tt, ts, mul, root, inverse, clip, shrink = math(step, 1)
            pool.wait_ge(b_sum, 1)
            root(nraw, s_n)
            clip(xn, nraw)
            pool.tensor_scalar(arg[:, 0:1], xn[:, 0:1], 1.0, None, ALU.mult).then_inc(b_arg, 1)
            step(pool.tensor_tensor(xinv[:, 0:1], xn[:, 0:1], c_minus[:, 0:1], ALU.pow))
            pool.wait_ge(b_tanh, 1)
            mul(co_a, tnh, xinv)
            step = steps(pool, "const2")
            tt, ts, mul, root, inverse, clip, shrink = math(step, 1)
            mul(nraw, co_a, nraw)
            shrink(scale_, nraw, extra)
            pool.tensor_tensor(co_c[:, 0:1], co_a[:, 0:1], scale_[:, 0:1], ALU.mult).then_inc(b_coef, 1)
            pool.wait_ge(b_ready, 1)

            inverse_std(1)

            def first_row(t, norm):
                for half in range(2):
                    stage((3 * t + 2) % NB, t, half, True, False)
                    if norm and half == 0:
                        inverse_std(t + 2)
            with pool.Fori(0, NB - 1) as t:
                first_row(t, True)
            first_row(NB - 1, False)

            with pool.Fori(*for_rows) as i:
                for t in range(NB):
                    j, task = pool.snap(block_of(i, t)), i * NB + t

                    def halves(use_t):
                        for half in range(2):
                            stage(j, task, half, True, use_t)
                            mid(i, 2 * t + half + 1)
                    if t == NB - 1:
                        halves(True)
                    else:
                        with pool.If(j < i):
                            halves(True)
                        with pool.Else():
                            halves(False)
            for t in range(NB):
                for half in range(2):
                    stage(t, NB * NB + t, half, False, True)
                    mid(NB, 2 * t + half + 1)
            with pool.Fori(0, NB - 1) as k:
                for t in range(NB - 1):
                    with pool.If(k >= t):
                        for half in range(2):
                            stage(p2_block(k, t), p2_tasks(k) + t, half, False, True)
                            final(k + 1, 2 * t + half + 1)
                    with pool.Else():
                        for half in range(2):
                            final(k + 1, 2 * t + half + 1)
            for at in range(10):
                final(NB, at)

        @block.tensor
        def _(pe):
            def product(acc, w_hi, w_lo, half, c, start):
                slot, w = c % SPLITS, bass.ts(c % HALF, F)
                last = None
                for n, (ws, a) in enumerate(((w_hi, a_hi), (w_lo, a_hi), (w_hi, a_lo))):
                    for b in range(BANKS):
                        last = pe.matmul(acc[:, bass.ts(b, BANK)], ws[:, half, w], a[:, slot, bass.ts(b, BANK)],
                                         start=start and n == 0, stop=False, skip_group_check=True)
                return last

            def half_block(task, half, use_h, use_t, start_h=False):
                pe.wait_ge(wlo_ready, task * 2 + half + 1)
                for c in range(half * HALF, (half + 1) * HALF):
                    pe.wait_ge(lo_ready, task * CH + c + 1)
                    last = None
                    if use_h:
                        last = product(hacc, hw_hi, hw_lo, half, c, start_h and c == 0)
                    if use_t:
                        last = product(tacc, tw_hi, tw_lo, half, c, False)
                    last.then_inc(chunk_used, 1)

            def zero_tacc():
                for b in range(BANKS):
                    pe.matmul(tacc[:, bass.ts(b, BANK)], zeros[:, :], zmove[:, :], start=True, stop=False,
                              skip_group_check=True)

            def transpose(src, signal):
                last = None
                for c in range(CH):
                    last = pe.transpose(pt[:, c, :], src(c), ident[:, :])
                last.then_inc(signal, 1)

            def mid(n, at):
                if at == 1:
                    transpose(lambda c: accT[:, bass.ts(c, P)], y_psum)
                if at == 4:
                    pe.wait_ge(h2_ready, n)
                    transpose(lambda c: z[:, c, :], h2t_psum)
                if at == 6:
                    pe.wait_ge(h2t_ready, n)
                    last = None
                    for c in range(CH):
                        last = pe.matmul(pt[:, c, :], accT[:, bass.ts(c, P)], w_sb[:, :], start=True, stop=True)
                    last.then_inc(mx_psum, 1)

            def final(n, at):
                if at == 1:
                    transpose(lambda c: accT[:, bass.ts(c, P)], s_psum)

            pe.wait_ge(zero_ready, 2)
            pe.wait_ge(pool_const, 1)
            for half in range(2):
                half_block(0, half, True, False, start_h=True)
            with pe.Fori(1, NB) as t:
                for half in range(2):
                    half_block(t, half, True, False)

            with pe.Fori(*for_rows) as i:
                pe.wait_ge(acc_saved, 2 * i)
                zero_tacc()
                for t in range(NB):
                    j, task = pe.snap(block_of(i, t)), i * NB + t

                    def halves(use_t):
                        for half in range(2):
                            half_block(task, half, True, use_t, start_h=t == 0)
                            mid(i, 2 * t + half + 1)
                    if t == NB - 1:
                        halves(True)
                    else:
                        with pe.If(j < i):
                            halves(True)
                        with pe.Else():
                            halves(False)
            pe.wait_ge(acc_saved, 2 * NB)
            zero_tacc()
            for t in range(NB):
                for half in range(2):
                    half_block(NB * NB + t, half, False, True)
                    mid(NB, 2 * t + half + 1)

            with pe.Fori(0, NB - 1) as k:
                wait_apart(pe, acc_saved, 2 * (NB + 1 + k))
                for b in range(BANKS):
                    pe.matmul(tacc[:, bass.ts(b, BANK)], ident[:, :], part[:, bass.ds(p2_row(k) * BLK + b * BANK, BANK)],
                              start=True, stop=False, skip_group_check=True)
                for t in range(NB - 1):
                    with pe.If(k >= t):
                        for half in range(2):
                            half_block(p2_tasks(k) + t, half, False, True)
                            final(k + 1, 2 * t + half + 1)
                    with pe.Else():
                        for half in range(2):
                            final(k + 1, 2 * t + half + 1)
            pe.wait_ge(acc_saved, 2 * (2 * NB))
            final(NB, 1)


def kernel(x, adj, L0_gnn_h, L1_gnn_weight, L1_gnn_bias):
    import concourse.bacc as bacc
    from concourse.bass_utils import run_bass_kernel_spmd

    def rows(a):
        return np.ascontiguousarray(a).reshape(NB, P, CH * F)

    blocks = np.asarray(adj).reshape(NB, P, CH, NB, P, LOADS, PAIR).transpose(0, 3, 5, 4, 6, 2, 1)
    arrays = {
        "x": rows(x),
        "adj": np.ascontiguousarray(blocks).reshape(NB, NB, LOADS, P, PAIR * BLK),
        "h0": rows(L0_gnn_h),
        "wt": np.ascontiguousarray(np.asarray(L1_gnn_weight).T),
        "bias": np.ascontiguousarray(L1_gnn_bias).reshape(1, F),
    }
    nc = bacc.Bacc("TRN2", target_bir_lowering=False, num_devices=1)
    args = [nc.dram_tensor(n, a.shape, F32, kind="ExternalInput").ap() for n, a in arrays.items()]
    out = nc.dram_tensor("out", (NB, P, CH * F), F32, kind="ExternalOutput").ap()
    build(nc, *args, out)
    r = run_bass_kernel_spmd(nc, [arrays], core_ids=[0])
    return r.results[0]["out"].reshape(N, F)
```

```python
from contextlib import ExitStack

import concourse.bass as bass
import numpy as np
from concourse import mybir
from concourse.alu_op_type import AluOpType as ALU

F32 = mybir.dt.float32
F32R = mybir.dt.float32r
ACT = mybir.ActivationFunctionType
AX = mybir.AxisListType

P = 128
N, F = 8192, 128
CH = 8
BLK = CH * P
NB = N // BLK
HALF = CH // 2
BANK = 512
BANKS = BLK // BANK
PAIR = 2
LOADS = CH // PAIR
SPLITS = 4
ALPHA = 0.1
LN_EPS = 1e-5
MIN_NORM = 1e-15
MAX_NORM = 1.0 - 0.004
ARTANH_MAX = float(np.float32(1.0 - 1e-7))
SERIES_BELOW = 0.25
SERIES = [1.0 / k for k in (13, 11, 9, 7, 5, 3)]

MID_ACT = {"normalise": 11, "square": 12, "h2T": 16, "mx": 21, "ln1": 22, "tanh": 31, "square_v": 41, "ln2": 46}
MID_DVE = {"x1": 6, "stats": 7, "xn": 14, "mx2": 23, "mxhb": 24, "dot": 25, "av": 37, "v": 39, "vn": 42, "tan": 53}
MID_PE = {"y": 1, "h2T": 10, "mx": 14}
MID_POOL = {"pre": 0, "rstd": 2, "xn": 4, "artanh1": 6, "mxn": 7, "ab": 8, "vn": 11, "c": 12}
FINAL_ACT = {"s": 7, "tanh1": 14, "ln": 17, "tanh2": 22}
FINAL_DVE = {"sn": 9, "r": 10, "rn": 11, "scale": 25, "out": 26}
FINAL_PE = {"s": 1}
FINAL_POOL = {"sn": 3, "series": 4, "nx": 4, "coef": 5}
SAVE = 3


def block_of(i, t):
    return (i + 3 * t + 2) % NB


def build(nc, x, adj, h0, wt, bias, out):
    with ExitStack() as ctx:
        def sb(name, shape, dt=F32):
            return ctx.enter_context(nc.sbuf_tensor(name, shape, dt))

        def sem(name):
            return ctx.enter_context(nc.semaphore(name))

        def psum(name, shape):
            return ctx.enter_context(nc.psum_tensor(name, shape, F32))

        x1_dram = nc.dram_tensor("x1_scratch", (NB, P, CH * F), F32, kind="Internal").ap()

        h = sb("h", [P, NB * CH * F])
        tan = sb("tan", [P, NB * CH * F])
        part = sb("part", [P, NB * BLK])
        raw = sb("raw", [P, CH, BLK])
        a_hi = sb("a_hi", [P, SPLITS, BLK], F32R)
        a_lo = sb("a_lo", [P, SPLITS, BLK], F32R)
        hw_hi = sb("hw_hi", [P, 2, HALF * F], F32R)
        hw_lo = sb("hw_lo", [P, 2, HALF * F], F32R)
        tw_hi = sb("tw_hi", [P, 2, HALF * F], F32R)
        tw_lo = sb("tw_lo", [P, 2, HALF * F], F32R)
        accT = sb("accT", [P, BLK])
        xin = sb("xin", [P, CH, F])
        h0in = sb("h0in", [P, CH, F])
        z = sb("z", [P, CH, F])
        v = sb("v", [P, CH, F])
        sq = sb("sq", [P, CH, F])
        accS = h[:, 0:BLK]
        ident = sb("ident", [P, P])
        zeros = sb("zeros", [P, P], mybir.dt.bfloat16)
        zmove = sb("zmove", [P, BANK], mybir.dt.bfloat16)
        w_sb = sb("w_sb", [P, F])
        hb = sb("hb", [P, 1, F])
        y2 = sb("y2", [P, 1])
        bstat = sb("bstat", [P, CH, 6])
        mv = sb("mv", [P, CH, 2])

        def small(name):
            return sb(name, [P, CH])

        c_mhalf, c_minus, c_eps = (small(n) for n in ("c_mhalf", "c_minus", "c_eps"))
        rstd, shift, s_x, s_m, s_d, s_v = small("rstd"), small("shift"), small("s_x"), small("s_m"), small("s_d"), small("s_v")
        s_n, s_r = small("s_n"), small("s_r")
        lnp, lnm, tnh = small("lnp"), small("lnm"), small("tnh")
        arg, co_a, co_b, co_c = (small(n) for n in ("arg", "co_a", "co_b", "co_c"))
        xinv, mnorm, minv, vinv, sinv, rnorm, at_ = (small(n) for n in
                                                     ("xinv", "mnorm", "minv", "vinv", "sinv", "rnorm", "at"))
        T = [small(f"tmp{n}") for n in range(4)]

        hacc = psum("hacc", [P, BLK])
        tacc = psum("tacc", [P, BLK])
        pt = psum("pt", [P, CH, F])

        const_in = sem("const_in")
        x_in = sem("x_in")
        adj_in = [sem(f"adj_in{q}") for q in range(LOADS)]
        rows_in = sem("rows_in")
        x1_in = sem("x1_in")
        x1_out = sem("x1_out")
        out_out = sem("out_out")
        hi_ready = sem("hi_ready")
        lo_ready = sem("lo_ready")
        chunk_used = sem("chunk_used")
        whi_ready = sem("whi_ready")
        wlo_ready = sem("wlo_ready")
        h_ready = sem("h_ready")
        acc_saved = sem("acc_saved")
        y_psum = sem("y_psum")
        pre_ready = sem("pre_ready")
        x1_ready = sem("x1_ready")
        h2_ready = sem("h2_ready")
        h2_squared = sem("h2_squared")
        xn_ready = sem("xn_ready")
        h2t_psum = sem("h2t_psum")
        h2t_ready = sem("h2t_ready")
        mx_psum = sem("mx_psum")
        mx_ready = sem("mx_ready")
        ln1_arg = sem("ln1_arg")
        ln1_ready = sem("ln1_ready")
        mx_sums = sem("mx_sums")
        tanh_arg = sem("tanh_arg")
        tanh_ready = sem("tanh_ready")
        mxhb_ready, a_ready, av_ready, bhb_ready = (sem(n) for n in ("mxhb", "a_ready", "av_ready", "bhb"))
        v_ready = sem("v_ready")
        v_squared = sem("v_squared")
        v_sum = sem("v_sum")
        ln2_arg = sem("ln2_arg")
        ln2_ready = sem("ln2_ready")
        c_ready = sem("c_ready")
        tan_ready = sem("tan_ready")
        stats_ready = sem("stats_ready")
        rstd_ready = sem("rstd_ready")
        s_psum = sem("s_psum")
        s_ready = sem("s_ready")
        r_squared, scaled = sem("r_squared"), sem("scaled")
        sn_ready, rn_ready = sem("sn_ready"), sem("rn_ready")
        f_arg1, f_tanh1 = sem("f_arg1"), sem("f_tanh1")
        f_arg2, f_ln = sem("f_arg2"), sem("f_ln")
        f_arg3, f_tanh2 = sem("f_arg3"), sem("f_tanh2")
        f_coef = sem("f_coef")
        out_ready = sem("out_ready")
        carried = sem("carried")
        pool_const = sem("pool_const")
        zero_ready = sem("zero_ready")
        b_sum, b_arg, b_tanh, b_coef, b_ready = (sem(f"bias_{n}") for n in ("sum", "arg", "tanh", "coef", "ready"))

        def wait_apart(eng, s, value):
            eng.wait_ge(s, value)
            if not isinstance(value, int):
                eng.sem_inc(carried)

        step_sems = {}

        def steps(eng, name):
            if name not in step_sems:
                step_sems[name] = sem("steps_" + name)
            s, n = step_sems[name], [0]
            eng.sem_clear(s)

            def step(ins):
                n[0] += 1
                ins.then_inc(s, 1)
                eng.wait_ge(s, n[0])

            return step

        def blk(i):
            return bass.ds(i * BLK, BLK)

        def half_blk(j, half):
            return bass.ds(j * BLK + half * (HALF * F), HALF * F)

        def flat(t3):
            return t3[:, :, :].rearrange("p c f -> p (c f)")

        def per_row(s):
            return s[:, :].rearrange("p (c o) -> p c o", o=1).to_broadcast([P, CH, F])

        rows_after_first = (1, NB)
        P2 = NB * NB
        PAIRS0 = P2 + NB
        PAIRS = (NB - 1) // 2
        LAST0 = PAIRS0 + PAIRS * NB
        LAST = NB // 2

        def small_row_block(p, t):
            return nc.s_assert_within(NB - 1 - p + t, 1, NB - 1,
                                      skip_runtime_bounds_check_because="that row has blocks t <= p only")

        def row_before(i, bank):
            return bass.ds((i - 1) * BLK + bank * BANK, BANK)

        def finals_of_pair(p, slot, final):
            if slot <= CH * NB // 2:
                final(2 * p + 1, slot, False)
            else:
                final(2 * p + 2, slot - CH * NB // 2, True)

        block = ctx.enter_context(nc.Block())

        @block.sync
        def _(sp):
            def load_block(i, j, task, waits=True):
                for q in range(LOADS):
                    if waits:
                        wait_apart(sp, lo_ready, (task - 1) * CH + (q + 1) * PAIR)
                    sp.dma_start(raw[:, q * PAIR:(q + 1) * PAIR, :].rearrange("p c n -> p (c n)"),
                                 adj[i, j, q]).then_inc(adj_in[q], 16)

            def load_rows(n):
                sp.dma_start(flat(xin), x[n - 1]).then_inc(rows_in, 16)
                sp.dma_start(flat(h0in), h0[n - 1]).then_inc(rows_in, 16)

            def store_x1(n):
                sp.wait_ge(x1_ready, n)
                sp.dma_start(x1_dram[n - 1], flat(xin)).then_inc(x1_out, 16)

            def x1_buffer(small):
                return z if small else xin

            def load_x1(row, small):
                sp.dma_start(flat(x1_buffer(small)), x1_dram[row]).then_inc(x1_in, 16)

            def store_out(n, row, small):
                sp.wait_ge(out_ready, n)
                sp.dma_start(out[row], flat(x1_buffer(small))).then_inc(out_out, 16)

            b = block_of(0, 0)
            sp.dma_start(h[:, b * BLK:(b + 1) * BLK], x[b]).then_inc(x_in, 16)
            load_block(0, b, 0, waits=False)
            sp.dma_start(hb[:, 0, :], bias.to_broadcast([P, F])).then_inc(const_in, 16)
            sp.dma_start(w_sb[:, :], wt).then_inc(const_in, 16)
            with sp.Fori(1, NB) as t:
                b = sp.snap((3 * t + 2) % NB)
                sp.wait_ge(x_in, 16 * t)
                sp.dma_start(h[:, blk(b)], x[b]).then_inc(x_in, 16)
                load_block(0, b, t)

            with sp.Fori(*rows_after_first) as i:
                load_rows(i)
                for t in range(NB):
                    load_block(i, block_of(i, t), i * NB + t)
                    if t == 2:
                        store_x1(i)
                    if t == NB - 2:
                        sp.wait_ge(x1_out, 16 * i)

            load_rows(NB)
            for t in range(NB):
                load_block(0, t, P2 + t)
                if t == 2:
                    store_x1(NB)
            sp.wait_ge(x1_out, 16 * NB)

            def pair_loads(p, t):
                if t == 0:
                    load_x1(p, False)
                if t == 5:
                    store_out(2 * p + 1, p, False)
                    load_x1(NB - 1 - p, True)

            with sp.Fori(0, PAIRS) as p:
                for t in range(NB):
                    if t == 0:
                        load_block(NB - 1 - p, NB - 1 - p, PAIRS0 + p * NB + t)
                    elif t < PAIRS:
                        with sp.If(p >= t):
                            load_block(NB - 1 - p, small_row_block(p, t), PAIRS0 + p * NB + t)
                        with sp.Else():
                            load_block(p + 1, t, PAIRS0 + p * NB + t)
                    else:
                        load_block(p + 1, t, PAIRS0 + p * NB + t)
                    pair_loads(p, t)
                store_out(2 * p + 2, NB - 1 - p, True)
                wait_apart(sp, out_out, 32 * p + 32)
            for t in range(NB - LAST):
                load_block(LAST, LAST + t, LAST0 + t)
                if t == 0:
                    load_x1(LAST - 1, False)
                    load_x1(LAST, True)
            store_out(NB - 1, LAST - 1, False)
            store_out(NB, LAST, True)
            sp.wait_ge(out_out, 16 * NB)

        @block.scalar
        def _(act):
            def stage(j, half, use_h, use_t):
                last = None
                if use_h:
                    last = act.activation(hw_hi[:, half, :], h[:, half_blk(j, half)], ACT.Copy)
                if use_t:
                    last = act.activation(tw_hi[:, half, :], tan[:, half_blk(j, half)], ACT.Copy)
                last.then_inc(whi_ready, 1)

            def chunk(task, c, first=False):
                if c % PAIR == 0:
                    act.wait_ge(adj_in[c // PAIR], (task + 1) * 16)
                if not first or c >= SPLITS:
                    act.wait_ge(chunk_used, task * CH + c - SPLITS + 1)
                act.activation(a_hi[:, c % SPLITS, :], raw[:, c, :], ACT.Copy).then_inc(hi_ready, 1)

            def save_acc(i):
                act.wait_ge(chunk_used, i * NB * CH)
                act.activation(accT[:, 0:BANK], hacc[:, 0:BANK], ACT.Copy, scale=1.0 - ALPHA)
                act.activation(part[:, row_before(i, 0)], tacc[:, 0:BANK], ACT.Copy).then_inc(acc_saved, 1)

            def normalise(dst, src, n, signal):
                act.wait_ge(rstd_ready, n)
                last = None
                for c in range(CH):
                    last = act.activation(dst[:, c, :], src[:, c, :], ACT.Relu, bias=shift[:, c:c + 1],
                                          scale=rstd[:, c:c + 1])
                last.then_inc(signal, 1)

            def norm_h(t):
                j = act.snap((3 * t + 2) % NB) if not isinstance(t, int) else block_of(0, t)
                hj = h[:, blk(j)].rearrange("p (c f) -> p c f", c=CH)
                normalise(hj, hj, t + 1, h_ready)

            def ln_pair(n, arg_sem, done_sem):
                act.wait_ge(arg_sem, n)
                act.activation(lnp[:, :], arg[:, :], ACT.Ln, bias=1.0, scale=1.0)
                act.activation(lnm[:, :], arg[:, :], ACT.Ln, bias=1.0, scale=-1.0).then_inc(done_sem, 1)

            def tanh(n, arg_sem, done_sem):
                act.wait_ge(arg_sem, n)
                act.activation(tnh[:, :], arg[:, :], ACT.Tanh).then_inc(done_sem, 1)

            def mid(n, slot):
                if slot == MID_ACT["normalise"]:
                    normalise(z, xin, NB + n, h2_ready)
                if slot == MID_ACT["square"]:
                    act.wait_ge(h2_ready, n)
                    act.activation(flat(sq), flat(z), ACT.Square).then_inc(h2_squared, 1)
                if slot == MID_ACT["h2T"]:
                    act.wait_ge(h2t_psum, n)
                    act.activation(accT[:, :], flat(pt), ACT.Copy).then_inc(h2t_ready, 1)
                if slot == MID_ACT["mx"]:
                    act.wait_ge(mx_psum, n)
                    act.activation(flat(sq), flat(pt), ACT.Square)
                    act.activation(flat(v), flat(pt), ACT.Copy).then_inc(mx_ready, 1)
                if slot == MID_ACT["ln1"]:
                    ln_pair(n, ln1_arg, ln1_ready)
                if slot == MID_ACT["tanh"]:
                    tanh(n, tanh_arg, tanh_ready)
                if slot == MID_ACT["square_v"]:
                    act.wait_ge(v_ready, n)
                    act.activation(flat(sq), flat(v), ACT.Square).then_inc(v_squared, 1)
                if slot == MID_ACT["ln2"]:
                    ln_pair(n, ln2_arg, ln2_ready)

            def final(n, slot, small):
                if slot == FINAL_ACT["s"]:
                    act.wait_ge(s_psum, n)
                    act.activation(flat(sq), flat(pt), ACT.Square)
                    act.activation(flat(v), flat(pt), ACT.Copy).then_inc(s_ready, 1)
                if slot == FINAL_ACT["tanh1"]:
                    tanh(n, f_arg1, f_tanh1)
                if slot == FINAL_ACT["ln"]:
                    ln_pair(n, f_arg2, f_ln)
                if slot == FINAL_ACT["tanh2"]:
                    tanh(n, f_arg3, f_tanh2)

            def first_row(t, norm, first=False):
                act.wait_ge(h_ready, t + 1)
                for c in range(CH):
                    if c % HALF == 0:
                        stage(block_of(0, t), c // HALF, True, False)
                    chunk(t, c, first)
                    if norm and c == CH - 2:
                        norm_h(t + 1)
            norm_h(0)
            first_row(0, True, True)
            act.wait_ge(b_arg, 1)
            act.activation(tnh[:, 0:1], arg[:, 0:1], ACT.Tanh).then_inc(b_tanh, 1)
            with act.Fori(1, NB - 1) as t:
                first_row(t, True)
            first_row(NB - 1, False)

            with act.Fori(*rows_after_first) as i:
                for t in range(NB):
                    j, task = act.snap(block_of(i, t)), i * NB + t

                    def chunks(use_t):
                        for c in range(CH):
                            if use_t and c == 0:
                                act.wait_ge(tan_ready, i if t == NB - 1 else j + 1)
                            if c % HALF == 0:
                                stage(j, c // HALF, True, use_t)
                            if t == 0 and c == SAVE:
                                save_acc(i)
                            chunk(task, c)
                            mid(i, t * CH + c + 1)

                    if t == NB - 1:
                        chunks(True)
                    else:
                        with act.If(j < i):
                            chunks(True)
                        with act.Else():
                            chunks(False)

            for t in range(NB):
                act.wait_ge(tan_ready, NB if t == NB - 1 else NB - 1)
                for c in range(CH):
                    if c % HALF == 0:
                        stage(t, c // HALF, False, True)
                    if t == 0 and c == SAVE:
                        save_acc(NB)
                    chunk(P2 + t, c)
                    mid(NB, t * CH + c + 1)

            with act.Fori(0, PAIRS) as p:
                for t in range(NB):
                    def chunks(j):
                        for c in range(CH):
                            if c % HALF == 0:
                                stage(j, c // HALF, False, True)
                            chunk(PAIRS0 + p * NB + t, c)
                            finals_of_pair(p, t * CH + c + 1, final)
                    if t == 0:
                        chunks(NB - 1 - p)
                    elif t < PAIRS:
                        with act.If(p >= t):
                            chunks(small_row_block(p, t))
                        with act.Else():
                            chunks(t)
                    else:
                        chunks(t)
            for t in range(NB - LAST):
                for c in range(CH):
                    if c % HALF == 0:
                        stage(LAST + t, c // HALF, False, True)
                    chunk(LAST0 + t, c)
                    final(NB - 1, t * CH + c + 1, False)
            for slot in range(CH * LAST + 1):
                final(NB, slot, True)

        @block.vector
        def _(dve):
            def chunk(task, c):
                dve.wait_ge(hi_ready, task * CH + c + 1)
                dve.tensor_tensor(a_lo[:, c % SPLITS, :], raw[:, c, :],
                                  a_hi[:, c % SPLITS, :].bitcast(F32), ALU.subtract).then_inc(lo_ready, 1)

            def save_acc(i):
                dve.wait_ge(chunk_used, i * NB * CH)
                dve.tensor_scalar(accT[:, BANK:BLK], hacc[:, BANK:BLK], 1.0 - ALPHA, None, ALU.mult)
                dve.tensor_copy(part[:, row_before(i, 1)], tacc[:, BANK:BLK]).then_inc(acc_saved, 1)

            def save_sum(blocks, row, small):
                wait_apart(dve, chunk_used, blocks * CH)
                dst = accS if small else accT
                dve.tensor_tensor(dst[:, :], tacc[:, :], part[:, blk(row)], ALU.add).then_inc(acc_saved, 1)

            def stats(src):
                step = steps(dve, "stats")
                last = None
                for c in range(CH):
                    last = dve.bn_stats(bstat[:, c, :], src[:, c, :])
                step(last)
                for c in range(CH):
                    last = dve.bn_aggr(mv[:, c, :], bstat[:, c, :])
                last.then_inc(stats_ready, 1)

            def row_sums(dst, src):
                return dve.tensor_reduce(dst[:, :], src[:, :, :], AX.X, ALU.add)

            def stats_h(t):
                wait_apart(dve, x_in, 16 * (t + 1))
                j = dve.snap((3 * t + 2) % NB) if not isinstance(t, int) else block_of(0, t)
                stats(h[:, blk(j)].rearrange("p (c f) -> p c f", c=CH))

            def mid(n, slot):
                if slot == MID_DVE["x1"]:
                    dve.wait_ge(pre_ready, n)
                    dve.wait_ge(y_psum, n)
                    dve.tensor_tensor(xin[:, :, :], pt[:, :, :], xin[:, :, :], ALU.add).then_inc(x1_ready, 1)
                if slot == MID_DVE["stats"]:
                    wait_apart(dve, x1_ready, n)
                    stats(xin)
                if slot == MID_DVE["xn"]:
                    dve.wait_ge(h2_squared, n)
                    row_sums(s_x, sq).then_inc(xn_ready, 1)
                if slot == MID_DVE["mx2"]:
                    dve.wait_ge(mx_ready, n)
                    row_sums(s_m, sq)
                if slot == MID_DVE["mxhb"]:
                    dve.tensor_tensor(h0in[:, :, :], v[:, :, :], hb[:, :, :].to_broadcast([P, CH, F]),
                                      ALU.mult).then_inc(mxhb_ready, 1)
                if slot == MID_DVE["dot"]:
                    dve.wait_ge(mxhb_ready, n)
                    row_sums(s_d, h0in).then_inc(mx_sums, 1)
                if slot == MID_DVE["av"]:
                    dve.wait_ge(a_ready, n)
                    dve.tensor_tensor(v[:, :, :], v[:, :, :], per_row(co_a), ALU.mult).then_inc(av_ready, 1)
                if slot == MID_DVE["v"]:
                    dve.wait_ge(av_ready, n)
                    dve.wait_ge(bhb_ready, n)
                    dve.tensor_tensor(v[:, :, :], v[:, :, :], sq[:, :, :], ALU.add).then_inc(v_ready, 1)
                if slot == MID_DVE["vn"]:
                    dve.wait_ge(v_squared, n)
                    row_sums(s_v, sq).then_inc(v_sum, 1)
                if slot == MID_DVE["tan"]:
                    dve.wait_ge(c_ready, n)
                    tj = tan[:, blk(n - 1)].rearrange("p (c f) -> p c f", c=CH)
                    dve.tensor_tensor(tj, v[:, :, :], per_row(co_c), ALU.mult).then_inc(tan_ready, 1)

            def final(n, slot, small):
                x1 = z if small else xin
                if slot == FINAL_DVE["sn"]:
                    dve.wait_ge(s_ready, n)
                    row_sums(s_n, sq).then_inc(sn_ready, 1)
                if slot == FINAL_DVE["r"]:
                    dve.scalar_tensor_tensor(h0in[:, :, :], v[:, :, :], 0.0, v[:, :, :],
                                             ALU.max, ALU.mult).then_inc(r_squared, 1)
                if slot == FINAL_DVE["rn"]:
                    dve.wait_ge(r_squared, n)
                    row_sums(s_r, h0in).then_inc(rn_ready, 1)
                if slot == FINAL_DVE["scale"]:
                    dve.wait_ge(f_coef, n)
                    dve.scalar_tensor_tensor(v[:, :, :], v[:, :, :], 0.0, per_row(co_c),
                                             ALU.max, ALU.mult).then_inc(scaled, 1)
                if slot == FINAL_DVE["out"]:
                    dve.wait_ge(scaled, n)
                    dve.wait_ge(x1_in, 16 * n)
                    dve.tensor_tensor(x1[:, :, :], x1[:, :, :], v[:, :, :], ALU.add).then_inc(out_ready, 1)

            def first_row(t, norm):
                for c in range(CH):
                    chunk(t, c)
                    if norm and c == 1:
                        stats_h(t + 1)
            stats_h(0)
            step = steps(dve, "bias")
            dve.wait_ge(const_in, 32)
            step(dve.tensor_tensor(sq[:, 0, :], hb[:, 0, :], hb[:, 0, :], ALU.mult))
            dve.tensor_reduce(s_n[:, 0:1], sq[:, 0, :], AX.X, ALU.add).then_inc(b_sum, 1)
            first_row(0, True)
            step = steps(dve, "hb")
            dve.wait_ge(b_coef, 1)
            step(dve.tensor_scalar(hb[:, 0, :], hb[:, 0, :], co_c[:, 0:1], None, ALU.mult))
            step(dve.tensor_tensor(sq[:, 0, :], hb[:, 0, :], hb[:, 0, :], ALU.mult))
            dve.tensor_reduce(y2[:, 0:1], sq[:, 0, :], AX.X, ALU.add).then_inc(b_ready, 1)
            with dve.Fori(1, NB - 1) as t:
                first_row(t, True)
            first_row(NB - 1, False)

            with dve.Fori(*rows_after_first) as i:
                for t in range(NB):
                    for c in range(CH):
                        if t == 0 and c == SAVE:
                            save_acc(i)
                        chunk(i * NB + t, c)
                        mid(i, t * CH + c + 1)

            for t in range(NB):
                for c in range(CH):
                    if t == 0 and c == SAVE:
                        save_acc(NB)
                    chunk(P2 + t, c)
                    mid(NB, t * CH + c + 1)

            with dve.Fori(0, PAIRS) as p:
                for t in range(NB):
                    for c in range(CH):
                        if c == SAVE:
                            if t == 0:
                                save_sum(PAIRS0 + p * NB, p, False)
                            elif t <= PAIRS:
                                with dve.If(p == t - 1):
                                    save_sum(PAIRS0 + p * NB + t, NB - 1 - p, True)
                        chunk(PAIRS0 + p * NB + t, c)
                        finals_of_pair(p, t * CH + c + 1, final)
            for t in range(NB - LAST):
                for c in range(CH):
                    if t == 0 and c == SAVE:
                        save_sum(LAST0, LAST - 1, False)
                    chunk(LAST0 + t, c)
                    final(NB - 1, t * CH + c + 1, False)
            save_sum(LAST0 + NB - LAST, LAST, True)
            for slot in range(CH * LAST + 1):
                final(NB, slot, True)

        @block.gpsimd
        def _(pool):
            def stage(j, task, half, use_h, use_t):
                wait_apart(pool, whi_ready, task * 2 + half + 1)
                last = None
                if use_h:
                    last = pool.tensor_tensor(hw_lo[:, half, :], h[:, half_blk(j, half)],
                                              hw_hi[:, half, :].bitcast(F32), ALU.subtract)
                if use_t:
                    last = pool.tensor_tensor(tw_lo[:, half, :], tan[:, half_blk(j, half)],
                                              tw_hi[:, half, :].bitcast(F32), ALU.subtract)
                last.then_inc(wlo_ready, 1)

            def arithmetic(name, w=CH):
                step = steps(pool, name)

                def end(ins, done):
                    if done is None:
                        step(ins)
                    else:
                        ins.then_inc(done, 1)

                def tt(o, a, b, op, done=None):
                    end(pool.tensor_tensor(o[:, 0:w], a[:, 0:w], b[:, 0:w], op), done)

                def ts(o, a, s1, op1, s2=None, op2=None, done=None):
                    if op2 is None:
                        end(pool.tensor_scalar(o[:, 0:w], a[:, 0:w], s1, None, op1), done)
                    else:
                        end(pool.tensor_scalar(o[:, 0:w], a[:, 0:w], s1, s2, op1, op2), done)

                def mul(o, a, b, done=None):
                    tt(o, a, b, ALU.mult, done)

                def power(o, a, exponent, done=None):
                    tt(o, a, exponent, ALU.pow, done)

                def norms(inverse, norm, squares, norm_done=None):
                    ts(inverse, squares, MIN_NORM * MIN_NORM, ALU.max)
                    mnorm_sq = T[3]
                    ts(mnorm_sq, squares, MIN_NORM * MIN_NORM, ALU.max)
                    power(inverse, inverse, c_mhalf)
                    mul(norm, mnorm_sq, inverse, norm_done)

                return tt, ts, mul, power, norms

            series_sum, mask = T[0], T[1]

            def series(ops):
                tt, ts, mul, power, norms = ops
                ts(mask, arg, SERIES_BELOW, ALU.is_lt)
                square = T[2]
                mul(square, arg, arg)
                ts(series_sum, square, SERIES[0], ALU.mult, SERIES[1], ALU.add)
                for k in SERIES[2:]:
                    mul(series_sum, series_sum, square)
                    ts(series_sum, series_sum, k, ALU.add)
                mul(series_sum, series_sum, square)
                ts(series_sum, series_sum, 1.0, ALU.add)
                mul(series_sum, series_sum, arg)

            def artanh(ops, o):
                tt, ts, mul, power, norms = ops
                tt(o, lnp, lnm, ALU.subtract)
                ts(o, o, 0.5, ALU.mult)
                tt(series_sum, series_sum, o, ALU.subtract)
                mul(series_sum, series_sum, mask)
                tt(o, o, series_sum, ALU.add)

            def inverse_std(n):
                tt, ts, mul, power, norms = arithmetic("inverse_std")
                wait_apart(pool, stats_ready, n)
                step = steps(pool, "eps")
                step(pool.tensor_tensor(rstd[:, :], mv[:, :, 1], c_eps[:, :], ALU.add))
                power(rstd, rstd, c_mhalf)
                step(pool.tensor_tensor(shift[:, :], mv[:, :, 0], rstd[:, :], ALU.mult))
                ts(shift, shift, -1.0, ALU.mult, done=rstd_ready)

            def mid(n, at):
                if at == MID_POOL["pre"]:
                    step = steps(pool, "pre")
                    wait_apart(pool, rows_in, 32 * n)
                    step(pool.tensor_scalar(h0in[:, :, :], h0in[:, :, :], ALPHA, 0.0, ALU.mult, ALU.add))
                    pool.tensor_tensor(xin[:, :, :], h0in[:, :, :], xin[:, :, :], ALU.add).then_inc(pre_ready, 1)
                if at == MID_POOL["rstd"]:
                    inverse_std(NB + n)
                if at == MID_POOL["xn"]:
                    tt, ts, mul, power, norms = arithmetic("xn")
                    wait_apart(pool, xn_ready, n)
                    norms(xinv, mnorm, s_x)
                    ts(arg, mnorm, ARTANH_MAX, ALU.min, done=ln1_arg)
                if at == MID_POOL["artanh1"]:
                    ops = arithmetic("artanh1")
                    wait_apart(pool, ln1_ready, n)
                    series(ops)
                    artanh(ops, at_)
                    ops[2](xinv, at_, xinv)
                if at == MID_POOL["mxn"]:
                    tt, ts, mul, power, norms = arithmetic("mxn")
                    wait_apart(pool, mx_sums, n)
                    norms(minv, mnorm, s_m)
                    mul(arg, xinv, mnorm, done=tanh_arg)
                if at == MID_POOL["ab"]:
                    tt, ts, mul, power, norms = arithmetic("ab")
                    norm, r, xy, den = tnh, minv, T[0], T[1]
                    wait_apart(pool, tanh_ready, n)
                    ts(norm, tnh, MAX_NORM, ALU.min)
                    mul(r, norm, minv)
                    mul(norm, norm, norm)
                    step = steps(pool, "den")
                    step(pool.tensor_scalar(den[:, :], norm[:, :], y2[:, 0:1], None, ALU.mult))
                    mul(xy, r, s_d)
                    ts(xy, xy, 2.0, ALU.mult, 1.0, ALU.add)
                    tt(den, den, xy, ALU.add)
                    ts(den, den, MIN_NORM, ALU.max)
                    power(den, den, c_minus)
                    step(pool.tensor_scalar(xy[:, :], xy[:, :], y2[:, 0:1], None, ALU.add))
                    mul(xy, xy, r)
                    mul(co_a, xy, den, done=a_ready)
                    ts(norm, norm, -1.0, ALU.mult, 1.0, ALU.add)
                    mul(co_b, norm, den)
                    pool.tensor_tensor(sq[:, :, :], hb[:, :, :].to_broadcast([P, CH, F]), per_row(co_b),
                                       ALU.mult).then_inc(bhb_ready, 1)
                if at == MID_POOL["vn"]:
                    tt, ts, mul, power, norms = arithmetic("vn")
                    wait_apart(pool, v_sum, n)
                    norms(vinv, mnorm, s_v)
                    ts(arg, mnorm, MAX_NORM, ALU.min, done=ln2_arg)
                if at == MID_POOL["c"]:
                    ops = arithmetic("c")
                    wait_apart(pool, ln2_arg, n)
                    series(ops)
                    wait_apart(pool, ln2_ready, n)
                    artanh(ops, at_)
                    ops[2](co_c, at_, vinv, done=c_ready)

            def final(n, at, small):
                if at == FINAL_POOL["sn"]:
                    tt, ts, mul, power, norms = arithmetic("sn")
                    wait_apart(pool, sn_ready, n)
                    norms(sinv, arg, s_n, norm_done=f_arg1)
                    wait_apart(pool, rn_ready, n)
                    norms(xinv, rnorm, s_r)
                if at == FINAL_POOL["series"]:
                    ops = arithmetic("series")
                    wait_apart(pool, f_tanh1, n)
                    wait_apart(pool, f_arg1, n)
                    ops[1](arg, tnh, MAX_NORM, ALU.min, done=f_arg2)
                    wait_apart(pool, f_arg2, n)
                    series(ops)
                if at == FINAL_POOL["nx"]:
                    ops = arithmetic("nx")
                    tt, ts, mul, power, norms = ops
                    wait_apart(pool, f_ln, n)
                    artanh(ops, at_)
                    mul(co_a, at_, sinv)
                    mul(rnorm, rnorm, co_a)
                    ts(rnorm, rnorm, MIN_NORM, ALU.max)
                    ts(arg, rnorm, 1.0, ALU.mult, done=f_arg3)
                    power(rnorm, rnorm, c_minus)
                    mul(co_a, co_a, rnorm)
                if at == FINAL_POOL["coef"]:
                    tt, ts, mul, power, norms = arithmetic("coef")
                    wait_apart(pool, f_tanh2, n)
                    ts(tnh, tnh, MAX_NORM, ALU.min)
                    mul(co_c, tnh, co_a, done=f_coef)

            step = steps(pool, "const")
            step(pool.memset(c_mhalf[:, :], -0.5))
            step(pool.memset(c_eps[:, :], LN_EPS))
            step(pool.memset(c_minus[:, :], -1.0))
            pool.memset(zeros[:, :], 0.0).then_inc(zero_ready, 1)
            pool.memset(zmove[:, :], 0.0).then_inc(zero_ready, 1)
            inverse_std(1)
            step(pool.memset(ident[:, :], 0.0))
            pool.affine_select(out=ident[:, :], in_=ident[:, :], compare_op=ALU.not_equal, fill=1.0,
                               base=0, pattern=[[-1, P]], channel_multiplier=1).then_inc(pool_const, 1)

            def first_row(t, norm):
                for half in range(2):
                    stage((3 * t + 2) % NB, t, half, True, False)
                    if norm and half == 0:
                        inverse_std(t + 2)
            first_row(0, True)
            tt, ts, mul, power, norms = arithmetic("bias", 1)
            pool.wait_ge(b_sum, 1)
            norms(xinv, arg, s_n, norm_done=b_arg)
            pool.wait_ge(b_tanh, 1)
            ts(co_a, tnh, MAX_NORM, ALU.min)
            mul(co_c, co_a, xinv, done=b_coef)
            with pool.Fori(1, NB - 1) as t:
                first_row(t, True)
            first_row(NB - 1, False)
            pool.wait_ge(b_ready, 1)

            with pool.Fori(*rows_after_first) as i:
                for t in range(NB):
                    j, task = pool.snap(block_of(i, t)), i * NB + t

                    def halves(use_t):
                        for half in range(2):
                            stage(j, task, half, True, use_t)
                            mid(i, 2 * t + half)
                    if t == NB - 1:
                        halves(True)
                    else:
                        with pool.If(j < i):
                            halves(True)
                        with pool.Else():
                            halves(False)
            for t in range(NB):
                for half in range(2):
                    stage(t, P2 + t, half, False, True)
                    mid(NB, 2 * t + half)

            with pool.Fori(0, PAIRS) as p:
                for t in range(NB):
                    def halves(j):
                        for half in range(2):
                            stage(j, PAIRS0 + p * NB + t, half, False, True)
                            at = 2 * t + half
                            if at < NB:
                                final(2 * p + 1, at, False)
                            else:
                                final(2 * p + 2, at - NB, True)
                    if t == 0:
                        halves(NB - 1 - p)
                    elif t < PAIRS:
                        with pool.If(p >= t):
                            halves(small_row_block(p, t))
                        with pool.Else():
                            halves(t)
                    else:
                        halves(t)
            for t in range(NB - LAST):
                for half in range(2):
                    stage(LAST + t, LAST0 + t, half, False, True)
                    final(NB - 1, 2 * t + half, False)
            for at in range(NB):
                final(NB, at, True)

        @block.tensor
        def _(pe):
            def product(acc, w_hi, w_lo, half, c, start):
                slot, w = c % SPLITS, bass.ts(c % HALF, F)
                last = None
                for n, (ws, a) in enumerate(((w_hi, a_hi), (w_lo, a_hi), (w_hi, a_lo))):
                    for b in range(BANKS):
                        last = pe.matmul(acc[:, bass.ts(b, BANK)], ws[:, half, w], a[:, slot, bass.ts(b, BANK)],
                                         start=start and n == 0, stop=False, skip_group_check=True)
                return last

            def chunk(task, c, use_h, use_t, start_h=False):
                if c % HALF == 0:
                    pe.wait_ge(wlo_ready, task * 2 + c // HALF + 1)
                pe.wait_ge(lo_ready, task * CH + c + 1)
                last = None
                if use_h:
                    last = product(hacc, hw_hi, hw_lo, c // HALF, c, start_h and c == 0)
                if use_t:
                    last = product(tacc, tw_hi, tw_lo, c // HALF, c, False)
                last.then_inc(chunk_used, 1)

            def zero_tacc():
                for b in range(BANKS):
                    pe.matmul(tacc[:, bass.ts(b, BANK)], zeros[:, :], zmove[:, :], start=True, stop=False,
                              skip_group_check=True)

            def transpose(src, signal):
                last = None
                for c in range(CH):
                    last = pe.transpose(pt[:, c, :], src(c), ident[:, :])
                last.then_inc(signal, 1)

            def mid(n, slot):
                if slot == MID_PE["y"]:
                    transpose(lambda c: accT[:, bass.ts(c, P)], y_psum)
                if slot == MID_PE["h2T"]:
                    pe.wait_ge(h2_ready, n)
                    transpose(lambda c: z[:, c, :], h2t_psum)
                if slot == MID_PE["mx"]:
                    pe.wait_ge(h2t_ready, n)
                    last = None
                    for c in range(CH):
                        last = pe.matmul(pt[:, c, :], accT[:, bass.ts(c, P)], w_sb[:, :], start=True, stop=True)
                    last.then_inc(mx_psum, 1)

            def final(n, slot, small):
                if slot == FINAL_PE["s"]:
                    src = accS if small else accT
                    transpose(lambda c: src[:, bass.ts(c, P)], s_psum)

            pe.wait_ge(zero_ready, 2)
            pe.wait_ge(pool_const, 1)
            zero_tacc()
            for c in range(CH):
                chunk(0, c, True, False, start_h=True)
            pe.wait_ge(const_in, 32)
            with pe.Fori(1, NB) as t:
                for c in range(CH):
                    chunk(t, c, True, False)

            with pe.Fori(*rows_after_first) as i:
                pe.wait_ge(acc_saved, 2 * i)
                zero_tacc()
                for t in range(NB):
                    j, task = pe.snap(block_of(i, t)), i * NB + t

                    def chunks(use_t):
                        for c in range(CH):
                            chunk(task, c, True, use_t, start_h=t == 0)
                            mid(i, t * CH + c + 1)
                    if t == NB - 1:
                        chunks(True)
                    else:
                        with pe.If(j < i):
                            chunks(True)
                        with pe.Else():
                            chunks(False)
            pe.wait_ge(acc_saved, 2 * NB)
            zero_tacc()
            for t in range(NB):
                for c in range(CH):
                    chunk(P2 + t, c, False, True)
                    mid(NB, t * CH + c + 1)

            with pe.Fori(0, PAIRS) as p:
                for t in range(NB):
                    if t == 0:
                        wait_apart(pe, acc_saved, 2 * NB + 2 * p + 1)
                        zero_tacc()
                    elif t <= PAIRS:
                        with pe.If(p == t - 1):
                            wait_apart(pe, acc_saved, 2 * NB + 2 * p + 2)
                            zero_tacc()
                    for c in range(CH):
                        chunk(PAIRS0 + p * NB + t, c, False, True)
                        finals_of_pair(p, t * CH + c + 1, final)
            pe.wait_ge(acc_saved, 2 * NB + 2 * PAIRS + 1)
            zero_tacc()
            for t in range(NB - LAST):
                for c in range(CH):
                    chunk(LAST0 + t, c, False, True)
                    final(NB - 1, t * CH + c + 1, False)
            pe.wait_ge(acc_saved, 2 * NB + 2 * PAIRS + 2)
            final(NB, FINAL_PE["s"], True)


def kernel(x, adj, L0_gnn_h, L1_gnn_weight, L1_gnn_bias):
    import concourse.bacc as bacc
    from concourse.bass_utils import run_bass_kernel_spmd

    def rows(a):
        return np.ascontiguousarray(a).reshape(NB, P, CH * F)

    blocks = np.asarray(adj).reshape(NB, P, CH, NB, P, LOADS, PAIR).transpose(0, 3, 5, 4, 6, 2, 1)
    arrays = {
        "x": rows(x),
        "adj": np.ascontiguousarray(blocks).reshape(NB, NB, LOADS, P, PAIR * BLK),
        "h0": rows(L0_gnn_h),
        "wt": np.ascontiguousarray(np.asarray(L1_gnn_weight).T),
        "bias": np.ascontiguousarray(L1_gnn_bias).reshape(1, F),
    }
    nc = bacc.Bacc("TRN2", target_bir_lowering=False, num_devices=1)
    args = [nc.dram_tensor(n, a.shape, F32, kind="ExternalInput").ap() for n, a in arrays.items()]
    out = nc.dram_tensor("out", (NB, P, CH * F), F32, kind="ExternalOutput").ap()
    build(nc, *args, out)
    r = run_bass_kernel_spmd(nc, [arrays], core_ids=[0])
    return r.results[0]["out"].reshape(N, F)
```

```python
from contextlib import ExitStack

import concourse.bass as bass
import numpy as np
from concourse import mybir
from concourse.alu_op_type import AluOpType as ALU

F32 = mybir.dt.float32
F32R = mybir.dt.float32r
ACT = mybir.ActivationFunctionType
AX = mybir.AxisListType

P = 128
N, F = 8192, 128
CH = 8
BLK = CH * P
NB = N // BLK
HALF = CH // 2
BANK = 512
BANKS = BLK // BANK
PER_LOAD = 1
LOADS = CH // PER_LOAD
SPLITS = 4
ALPHA = 0.1
LN_EPS = 1e-5
MIN_NORM = 1e-15
MAX_NORM = 1.0 - 0.004
ARTANH_MAX = float(np.float32(1.0 - 1e-7))
SERIES_BELOW = 0.25
SERIES = [1.0 / k for k in (13, 11, 9, 7, 5, 3)]

MID_ACT = {"normalise": (14, 16), "square": 18, "h2T": 19, "ln1": 25,
           "mx": 26, "tanh": 30, "square_v": 42, "ln2": 50}
MID_DVE = {"x1": 5, "stats": (7, 9), "xn": 18, "mx2": 26, "av": 38, "vn": 44}
MID_PE = {"y": 1, "h2T": 16, "mx": 22}
MID_POOL = {"pre": 0, "rstd": 2, "xn": 5, "artanh1": 6, "mxn": 6,
            "ab": 8, "v": 9, "vn": 11, "c": 12}
FINAL_ACT = {"s": 6, "tanh1": 14, "ln": 18, "tanh2": 25}
FINAL_DVE = {"sn": 6, "r": 9, "rn": 12, "scale": 29}
FINAL_PE = {"s": 2}
FINAL_POOL = {"sn": 3, "series": 4, "nx": 5, "coef": 6, "out": 7}
NORM_H, STATS_H = (0, 5), (1, 4)
SAVE = 2
SAVE_BEFORE, SAVE_SMALL = (0, 1), (3, 6)


def block_of(i, t):
    return (i + 3 * t + 2) % NB


def build(nc, x, adj, h0, wt, bias, out):
    with ExitStack() as ctx:
        def sb(name, shape, dt=F32):
            return ctx.enter_context(nc.sbuf_tensor(name, shape, dt))

        def sem(name):
            return ctx.enter_context(nc.semaphore(name))

        def psum(name, shape):
            return ctx.enter_context(nc.psum_tensor(name, shape, F32))

        x1_dram = nc.dram_tensor("x1_scratch", (NB, P, CH * F), F32, kind="Internal").ap()

        h = sb("h", [P, NB * CH * F])
        tan = sb("tan", [P, NB * CH * F])
        part = sb("part", [P, NB * BLK])
        raw = sb("raw", [P, CH, BLK])
        a_hi = sb("a_hi", [P, SPLITS, BLK], F32R)
        a_lo = sb("a_lo", [P, SPLITS, BLK], F32R)
        hw_hi = sb("hw_hi", [P, 2, HALF * F], F32R)
        hw_lo = sb("hw_lo", [P, 2, HALF * F], F32R)
        tw_hi = sb("tw_hi", [P, 2, HALF * F], F32R)
        tw_lo = sb("tw_lo", [P, 2, HALF * F], F32R)
        accT = sb("accT", [P, BLK])
        xin = sb("xin", [P, CH, F])
        h0in = sb("h0in", [P, CH, F])
        z = sb("z", [P, CH, F])
        v = sb("v", [P, CH, F])
        sq = sb("sq", [P, CH, F])
        ident = sb("ident", [P, P])
        zeros = sb("zeros", [P, P], mybir.dt.bfloat16)
        zmove = sb("zmove", [P, BANK], mybir.dt.bfloat16)
        w_sb = sb("w_sb", [P, F])
        hb = sb("hb", [P, 1, F])
        w_hb = sb("w_hb", [P, 1])
        y2 = sb("y2", [P, 1])
        bstat = sb("bstat", [P, CH, 6])
        mv = sb("mv", [P, CH, 2])

        def small(name):
            return sb(name, [P, CH])

        c_mhalf, c_minus, c_eps, c_one = (small(n) for n in ("c_mhalf", "c_minus", "c_eps", "c_one"))
        unused = small("unused")
        rstd, shift = small("rstd"), small("shift")
        s_x, s_m, s_d, s_v, s_n, s_r = (small(n) for n in ("s_x", "s_m", "s_d", "s_v", "s_n", "s_r"))
        lnp, lnm, tnh = small("lnp"), small("lnm"), small("tnh")
        arg, co_a, co_b, co_c = (small(n) for n in ("arg", "co_a", "co_b", "co_c"))
        xinv, mnorm, minv, vinv, sinv, rnorm, at_ = (small(n) for n in
                                                     ("xinv", "mnorm", "minv", "vinv", "sinv", "rnorm", "at"))
        T = [small(f"tmp{n}") for n in range(4)]

        hacc = psum("hacc", [P, BLK])
        tacc = psum("tacc", [P, BLK])
        pt = psum("pt", [P, CH, F])
        dots = psum("dots", [P, CH])

        const_in = sem("const_in")
        x_in = sem("x_in")
        adj_in = [sem(f"adj_in{q}") for q in range(LOADS)]
        rows_in = sem("rows_in")
        x1_in = sem("x1_in")
        stored = sem("stored")
        hi_ready = sem("hi_ready")
        lo_ready = sem("lo_ready")
        chunk_used = sem("chunk_used")
        whi_ready = sem("whi_ready")
        wlo_ready = sem("wlo_ready")
        h_ready = sem("h_ready")
        hacc_saved = sem("hacc_saved")
        acc_saved = sem("acc_saved")
        pre_ready = sem("pre_ready")
        y_psum = sem("y_psum")
        x1_ready = sem("x1_ready")
        h2_ready = sem("h2_ready")
        h2_squared = sem("h2_squared")
        xn_ready = sem("xn_ready")
        h2t_psum = sem("h2t_psum")
        h2t_ready = sem("h2t_ready")
        mx_psum = sem("mx_psum")
        mx_ready = sem("mx_ready")
        mx_sums = sem("mx_sums")
        ln1_arg = sem("ln1_arg")
        ln1_ready = sem("ln1_ready")
        tanh_arg = sem("tanh_arg")
        tanh_ready = sem("tanh_ready")
        a_ready = sem("a_ready")
        av_ready = sem("av_ready")
        bhb_ready = sem("bhb_ready")
        v_ready = sem("v_ready")
        v_squared = sem("v_squared")
        v_sum = sem("v_sum")
        ln2_arg = sem("ln2_arg")
        ln2_ready = sem("ln2_ready")
        tan_ready = sem("tan_ready")
        stats_ready = sem("stats_ready")
        rstd_ready = sem("rstd_ready")
        s_psum = sem("s_psum")
        s_ready = sem("s_ready")
        sn_ready = sem("sn_ready")
        r_squared = sem("r_squared")
        rn_ready = sem("rn_ready")
        f_arg1, f_tanh1 = sem("f_arg1"), sem("f_tanh1")
        f_rnorm = sem("f_rnorm")
        f_arg2, f_ln = sem("f_arg2"), sem("f_ln")
        f_arg3, f_tanh2 = sem("f_arg3"), sem("f_tanh2")
        f_coef = sem("f_coef")
        scaled = sem("scaled")
        out_ready = sem("out_ready")
        carried = sem("carried")
        pool_const = sem("pool_const")
        zero_ready = sem("zero_ready")
        b_sum, b_arg, b_tanh, b_coef, b_ready = (sem(f"bias_{n}") for n in ("sum", "arg", "tanh", "coef", "ready"))

        def wait_apart(eng, s, value):
            eng.wait_ge(s, value)
            if not isinstance(value, int):
                eng.sem_inc(carried)

        step_sems = {}

        def steps(eng, name):
            if name not in step_sems:
                step_sems[name] = sem("steps_" + name)
            s, n = step_sems[name], [0]
            eng.sem_clear(s)

            def step(ins):
                n[0] += 1
                ins.then_inc(s, 1)
                eng.wait_ge(s, n[0])

            return step

        def blk(i):
            return bass.ds(i * BLK, BLK)

        def half_blk(j, half):
            return bass.ds(j * BLK + half * (HALF * F), HALF * F)

        def flat(t3):
            return t3[:, :, :].rearrange("p c f -> p (c f)")

        def rows_of(columns):
            return columns.rearrange("p (c f) -> p c f", c=CH)

        def per_row(s):
            return s[:, :].rearrange("p (c o) -> p c o", o=1).to_broadcast([P, CH, F])

        rows_after_first = (1, NB)
        P2 = NB * NB
        PAIRS0 = P2 + NB
        PAIRS = (NB - 1) // 2
        LAST0 = PAIRS0 + PAIRS * NB
        LAST = NB // 2

        def small_row_block(p, t):
            return nc.s_assert_within(NB - 1 - p + t, 1, NB - 1,
                                      skip_runtime_bounds_check_because="that row has blocks t <= p only")

        def row_before(i, bank):
            return bass.ds((i - 1) * BLK + bank * BANK, BANK)

        def finals_of_pair(p, slot, final):
            if slot <= CH * NB // 2:
                final(2 * p + 1, slot, p)
            else:
                final(2 * p + 2, slot - CH * NB // 2, NB - 1 - p)

        def x1_of(n):
            last = isinstance(n, int) and n == NB
            return rows_of(h[:, blk(NB - 1)]) if last else xin

        def arithmetic(eng, name, w=CH):
            step = steps(eng, name)

            def end(ins, done):
                if done is None:
                    step(ins)
                else:
                    ins.then_inc(done, 1)

            def tt(o, a, b, op, done=None):
                end(eng.tensor_tensor(o[:, 0:w], a[:, 0:w], b[:, 0:w], op), done)

            def ts(o, a, s1, op1, s2=None, op2=None, done=None):
                if op2 is None:
                    end(eng.tensor_scalar(o[:, 0:w], a[:, 0:w], s1, None, op1), done)
                else:
                    end(eng.tensor_scalar(o[:, 0:w], a[:, 0:w], s1, s2, op1, op2), done)

            def mul(o, a, b, done=None):
                tt(o, a, b, ALU.mult, done)

            def power(o, a, exponent, done=None):
                tt(o, a, exponent, ALU.pow, done)

            def norms(inverse, norm, squares, norm_done=None):
                ts(inverse, squares, MIN_NORM * MIN_NORM, ALU.max)
                mnorm_sq = T[3]
                ts(mnorm_sq, squares, MIN_NORM * MIN_NORM, ALU.max)
                power(inverse, inverse, c_mhalf)
                mul(norm, mnorm_sq, inverse, norm_done)

            return tt, ts, mul, power, norms

        series_sum, mask = T[0], T[1]

        def series(ops):
            tt, ts, mul, power, norms = ops
            ts(mask, arg, SERIES_BELOW, ALU.is_lt)
            square = T[2]
            mul(square, arg, arg)
            ts(series_sum, square, SERIES[0], ALU.mult, SERIES[1], ALU.add)
            for k in SERIES[2:]:
                mul(series_sum, series_sum, square)
                ts(series_sum, series_sum, k, ALU.add)
            mul(series_sum, series_sum, square)
            ts(series_sum, series_sum, 1.0, ALU.add)
            mul(series_sum, series_sum, arg)

        def artanh(ops, o):
            tt, ts, mul, power, norms = ops
            tt(o, lnp, lnm, ALU.subtract)
            ts(o, o, 0.5, ALU.mult)
            tt(series_sum, series_sum, o, ALU.subtract)
            mul(series_sum, series_sum, mask)
            tt(o, o, series_sum, ALU.add)

        def final_norms(eng, n, at, row):
            if at in ("sn", FINAL_POOL["sn"]):
                tt, ts, mul, power, norms = arithmetic(eng, "sn")
                wait_apart(eng, sn_ready, n)
                norms(sinv, arg, s_n, norm_done=f_arg1)
                wait_apart(eng, rn_ready, n)
                norms(xinv, rnorm, s_r, norm_done=f_rnorm)
            if at in ("series", FINAL_POOL["series"]):
                ops = arithmetic(eng, "series")
                wait_apart(eng, f_tanh1, n)
                wait_apart(eng, f_arg1, n)
                ops[1](arg, tnh, MAX_NORM, ALU.min, done=f_arg2)
                wait_apart(eng, f_arg2, n)
                series(ops)
            if at in ("nx", FINAL_POOL["nx"]):
                ops = arithmetic(eng, "nx")
                tt, ts, mul, power, norms = ops
                wait_apart(eng, f_rnorm, n)
                wait_apart(eng, f_ln, n)
                artanh(ops, at_)
                mul(co_a, at_, sinv)
                mul(rnorm, rnorm, co_a)
                ts(rnorm, rnorm, MIN_NORM, ALU.max)
                ts(arg, rnorm, 1.0, ALU.mult, done=f_arg3)
                if eng is nc.vector:
                    steps(eng, "reciprocal")(eng.reciprocal(rnorm[:, :], rnorm[:, :]))
                else:
                    power(rnorm, rnorm, c_minus)
                mul(co_a, co_a, rnorm)
            if at in ("coef", FINAL_POOL["coef"]):
                tt, ts, mul, power, norms = arithmetic(eng, "coef")
                wait_apart(eng, f_tanh2, n)
                ts(tnh, tnh, MAX_NORM, ALU.min)
                mul(co_c, tnh, co_a, done=f_coef)
            if at in ("out", FINAL_POOL["out"]):
                wait_apart(eng, scaled, n)
                eng.wait_ge(x1_in, 16 * (NB - 1))
                x1 = rows_of(h[:, blk(row)])
                eng.tensor_tensor(x1, x1, v[:, :, :], ALU.add).then_inc(out_ready, 1)

        block = ctx.enter_context(nc.Block())

        @block.sync
        def _(sp):
            def load_block(i, j, task, waits=True, loads=range(LOADS)):
                for q in loads:
                    if waits:
                        wait_apart(sp, lo_ready, (task - 1) * CH + (q + 1) * PER_LOAD)
                    sp.dma_start(raw[:, q * PER_LOAD:(q + 1) * PER_LOAD, :].rearrange("p c n -> p (c n)"),
                                 adj[i, j, q]).then_inc(adj_in[q], 16)

            def load_rows(n):
                sp.dma_start(flat(xin), x[n - 1]).then_inc(rows_in, 16)
                sp.dma_start(flat(h0in), h0[n - 1]).then_inc(rows_in, 16)

            def store_x1(n):
                sp.wait_ge(x1_ready, n)
                sp.dma_start(x1_dram[n - 1], flat(xin)).then_inc(stored, 16)

            def load_x1(row):
                sp.dma_start(h[:, blk(row)], x1_dram[row]).then_inc(x1_in, 16)

            def store_out(n, row):
                wait_apart(sp, out_ready, n)
                sp.dma_start(out[row], h[:, blk(row)]).then_inc(stored, 16)

            def load_x(t):
                b = sp.snap((3 * t + 2) % NB) if not isinstance(t, int) else block_of(0, t)
                sp.dma_start(h[:, blk(b)], x[b]).then_inc(x_in, 16)

            load_x(0)
            load_block(0, block_of(0, 0), 0, waits=False, loads=range(1))
            sp.wait_ge(x_in, 16)
            load_x(1)
            load_block(0, block_of(0, 0), 0, waits=False, loads=range(1, LOADS))
            sp.wait_ge(x_in, 32)
            load_x(2)
            sp.dma_start(hb[:, 0, :], bias.to_broadcast([P, F])).then_inc(const_in, 16)
            sp.dma_start(w_sb[:, :], wt).then_inc(const_in, 16)
            with sp.Fori(1, NB - 2) as t:
                wait_apart(sp, x_in, 16 * t + 32)
                load_x(t + 2)
                load_block(0, sp.snap((3 * t + 2) % NB), t)
            load_block(0, block_of(0, NB - 2), NB - 2)
            load_rows(1)
            load_block(0, block_of(0, NB - 1), NB - 1)

            with sp.Fori(*rows_after_first) as i:
                for t in range(NB):
                    load_block(i, block_of(i, t), i * NB + t)
                    if 0 < t and block_of(NB - 1, t - 1) < NB - 1:
                        with sp.If(i == NB - 1):
                            wait_apart(sp, wlo_ready, (i * NB + t) * 2)
                            load_x1(block_of(NB - 1, t - 1))
                    if t == 2:
                        store_x1(i)
                    if t == NB - 2:
                        wait_apart(sp, stored, 16 * i)
                        load_rows(i + 1)

            for t in range(NB):
                load_block(0, t, P2 + t)
                if t == 0:
                    sp.wait_ge(wlo_ready, P2 * 2)
                    load_x1(NB - 2)

            def pair_rows(p, t):
                if t == 2:
                    with sp.If(p >= 1):
                        row = nc.s_assert_within(NB - p, 1, NB - 1, skip_runtime_bounds_check_because="p >= 1")
                        store_out(2 * p, row)
                if t == 5:
                    store_out(2 * p + 1, p)

            with sp.Fori(0, PAIRS) as p:
                for t in range(NB):
                    if t == 0:
                        load_block(NB - 1 - p, NB - 1 - p, PAIRS0 + p * NB + t)
                    elif t < PAIRS:
                        with sp.If(p >= t):
                            load_block(NB - 1 - p, small_row_block(p, t), PAIRS0 + p * NB + t)
                        with sp.Else():
                            load_block(p + 1, t, PAIRS0 + p * NB + t)
                    else:
                        load_block(p + 1, t, PAIRS0 + p * NB + t)
                    pair_rows(p, t)
            for t in range(NB - LAST):
                load_block(LAST, LAST + t, LAST0 + t)
                if t == 1:
                    store_out(2 * PAIRS, NB - PAIRS)
            store_out(NB - 1, LAST - 1)
            store_out(NB, LAST)
            sp.wait_ge(stored, 16 * (2 * NB - 1))

        @block.scalar
        def _(act):
            def stage(j, half, use_h, use_t):
                last = None
                if use_h:
                    last = act.activation(hw_hi[:, half, :], h[:, half_blk(j, half)], ACT.Copy)
                if use_t:
                    last = act.activation(tw_hi[:, half, :], tan[:, half_blk(j, half)], ACT.Copy)
                last.then_inc(whi_ready, 1)

            def chunk(task, c, first=False):
                if c % PER_LOAD == 0:
                    act.wait_ge(adj_in[c // PER_LOAD], (task + 1) * 16)
                if not first or c >= SPLITS:
                    act.wait_ge(chunk_used, task * CH + c - SPLITS + 1)
                act.activation(a_hi[:, c % SPLITS, :], raw[:, c, :], ACT.Copy).then_inc(hi_ready, 1)

            def save_acc(i):
                act.wait_ge(chunk_used, i * NB * CH)
                act.activation(accT[:, 0:BANK], hacc[:, 0:BANK], ACT.Copy,
                               scale=1.0 - ALPHA).then_inc(hacc_saved, 1)
                act.activation(part[:, row_before(i, 0)], tacc[:, 0:BANK], ACT.Copy).then_inc(acc_saved, 1)

            def normalise(dst, src, n, signal, chunks=range(CH)):
                act.wait_ge(rstd_ready, n)
                last = None
                for c in chunks:
                    last = act.activation(dst[:, c, :], src[:, c, :], ACT.Relu, bias=shift[:, c:c + 1],
                                          scale=rstd[:, c:c + 1])
                if c == CH - 1:
                    last.then_inc(signal, 1)

            def norm_h(t, chunks=range(CH)):
                j = act.snap((3 * t + 2) % NB) if not isinstance(t, int) else block_of(0, t)
                hj = h[:, blk(j)].rearrange("p (c f) -> p c f", c=CH)
                normalise(hj, hj, t + 1, h_ready, chunks)

            def ln_pair(n, arg_sem, done_sem):
                act.wait_ge(arg_sem, n)
                act.activation(lnp[:, :], arg[:, :], ACT.Ln, bias=1.0, scale=1.0)
                act.activation(lnm[:, :], arg[:, :], ACT.Ln, bias=1.0, scale=-1.0).then_inc(done_sem, 1)

            def tanh(n, arg_sem, done_sem):
                act.wait_ge(arg_sem, n)
                act.activation(tnh[:, :], arg[:, :], ACT.Tanh).then_inc(done_sem, 1)

            def mid(n, slot):
                for q, place in enumerate(MID_ACT["normalise"]):
                    if slot == place:
                        normalise(z, x1_of(n), NB + n, h2_ready, range(q * HALF, (q + 1) * HALF))
                if slot == MID_ACT["square"]:
                    act.wait_ge(h2_ready, n)
                    act.activation(flat(sq), flat(z), ACT.Square).then_inc(h2_squared, 1)
                if slot == MID_ACT["h2T"]:
                    act.wait_ge(h2t_psum, n)
                    act.activation(accT[:, :], flat(pt), ACT.Copy).then_inc(h2t_ready, 1)
                if slot == MID_ACT["mx"]:
                    act.wait_ge(mx_psum, n)
                    act.activation(flat(sq), flat(pt), ACT.Square).then_inc(mx_ready, 1)
                if slot == MID_ACT["ln1"]:
                    ln_pair(n, ln1_arg, ln1_ready)
                if slot == MID_ACT["tanh"]:
                    tanh(n, tanh_arg, tanh_ready)
                if slot == MID_ACT["square_v"]:
                    act.wait_ge(v_ready, n)
                    act.activation(flat(sq), flat(v), ACT.Square).then_inc(v_squared, 1)
                if slot == MID_ACT["ln2"]:
                    ln_pair(n, ln2_arg, ln2_ready)

            def final(n, slot, row):
                if slot in ("s", FINAL_ACT["s"]):
                    act.wait_ge(s_psum, n)
                    act.activation(flat(sq), flat(pt), ACT.Square).then_inc(s_ready, 1)
                if slot in ("tanh1", FINAL_ACT["tanh1"]):
                    tanh(n, f_arg1, f_tanh1)
                if slot in ("ln", FINAL_ACT["ln"]):
                    ln_pair(n, f_arg2, f_ln)
                if slot in ("tanh2", FINAL_ACT["tanh2"]):
                    tanh(n, f_arg3, f_tanh2)

            def first_row(t, norm, first=False):
                act.wait_ge(h_ready, t + 1)
                for c in range(CH):
                    if c % HALF == 0:
                        stage(block_of(0, t), c // HALF, True, False)
                    chunk(t, c, first)
                    if norm and c in NORM_H:
                        q = NORM_H.index(c)
                        norm_h(t + 1, range(q * HALF, (q + 1) * HALF))
            norm_h(0)
            first_row(0, True, True)
            with act.Fori(1, NB - 1) as t:
                first_row(t, True)
            act.wait_ge(b_arg, 1)
            act.activation(tnh[:, 0:1], arg[:, 0:1], ACT.Tanh).then_inc(b_tanh, 1)
            first_row(NB - 1, False)

            with act.Fori(*rows_after_first) as i:
                for t in range(NB):
                    j, task = act.snap(block_of(i, t)), i * NB + t

                    def chunks(use_t):
                        for c in range(CH):
                            if use_t and c == 0:
                                act.wait_ge(tan_ready, i if t == NB - 1 else j + 1)
                            if c % HALF == 0:
                                stage(j, c // HALF, True, use_t)
                            if t == 0 and c == SAVE:
                                save_acc(i)
                            chunk(task, c)
                            mid(i, t * CH + c + 1)

                    if t == NB - 1:
                        chunks(True)
                    else:
                        with act.If(j < i):
                            chunks(True)
                        with act.Else():
                            chunks(False)

            for t in range(NB):
                act.wait_ge(tan_ready, NB if t == NB - 1 else NB - 1)
                for c in range(CH):
                    if c % HALF == 0:
                        stage(t, c // HALF, False, True)
                    if t == 0 and c == SAVE:
                        save_acc(NB)
                    chunk(P2 + t, c)
                    mid(NB, t * CH + c + 1)

            with act.Fori(0, PAIRS) as p:
                for t in range(NB):
                    def chunks(j):
                        for c in range(CH):
                            if c % HALF == 0:
                                stage(j, c // HALF, False, True)
                            chunk(PAIRS0 + p * NB + t, c)
                            finals_of_pair(p, t * CH + c + 1, final)
                    if t == 0:
                        chunks(NB - 1 - p)
                    elif t < PAIRS:
                        with act.If(p >= t):
                            chunks(small_row_block(p, t))
                        with act.Else():
                            chunks(t)
                    else:
                        chunks(t)
            for t in range(NB - LAST):
                for c in range(CH):
                    if c % HALF == 0:
                        stage(LAST + t, c // HALF, False, True)
                    chunk(LAST0 + t, c)
                    final(NB - 1, t * CH + c + 1, LAST - 1)
            for n, (place, function) in enumerate((("s", ACT.Tanh), ("tanh1", ACT.Ln), ("ln", ACT.Tanh))):
                final(NB, place, LAST)
                act.activation(unused[:, n:n + 1], c_one[:, n:n + 1], function)
            final(NB, "tanh2", LAST)

        @block.vector
        def _(dve):
            def chunk(task, c):
                dve.wait_ge(hi_ready, task * CH + c + 1)
                dve.tensor_tensor(a_lo[:, c % SPLITS, :], raw[:, c, :],
                                  a_hi[:, c % SPLITS, :].bitcast(F32), ALU.subtract).then_inc(lo_ready, 1)

            def save_acc(i):
                dve.wait_ge(chunk_used, i * NB * CH)
                dve.tensor_scalar(accT[:, BANK:BLK], hacc[:, BANK:BLK], 1.0 - ALPHA, None,
                                  ALU.mult).then_inc(hacc_saved, 1)
                dve.tensor_copy(part[:, row_before(i, 1)], tacc[:, BANK:BLK]).then_inc(acc_saved, 1)

            def save_sum(blocks, row, acc):
                wait_apart(dve, chunk_used, blocks * CH)
                dve.tensor_tensor(accT[:, :], acc[:, :], part[:, blk(row)], ALU.add).then_inc(acc_saved, 1)

            def stats(src, chunks=range(CH)):
                step = steps(dve, "stats")
                last = None
                for c in chunks:
                    last = dve.bn_stats(bstat[:, c, :], src[:, c, :])
                step(last)
                for c in chunks:
                    last = dve.bn_aggr(mv[:, c, :], bstat[:, c, :])
                if c == CH - 1:
                    last.then_inc(stats_ready, 1)

            def row_sums(dst, src):
                return dve.tensor_reduce(dst[:, :], src[:, :, :], AX.X, ALU.add)

            def stats_h(t, chunks=range(CH)):
                wait_apart(dve, x_in, 16 * (t + 1))
                if not isinstance(t, int) or t > 0:
                    wait_apart(dve, rstd_ready, t)
                j = dve.snap((3 * t + 2) % NB) if not isinstance(t, int) else block_of(0, t)
                stats(h[:, blk(j)].rearrange("p (c f) -> p c f", c=CH), chunks)

            def mid(n, slot):
                if slot == MID_DVE["x1"]:
                    dve.wait_ge(pre_ready, n)
                    dve.wait_ge(y_psum, n)
                    dve.tensor_tensor(x1_of(n)[:, :, :], pt[:, :, :], xin[:, :, :], ALU.add).then_inc(x1_ready, 1)
                for q, place in enumerate(MID_DVE["stats"]):
                    if slot == place:
                        wait_apart(dve, x1_ready, n)
                        stats(x1_of(n), range(q * HALF, (q + 1) * HALF))
                if slot == MID_DVE["xn"]:
                    dve.wait_ge(h2_squared, n)
                    row_sums(s_x, sq).then_inc(xn_ready, 1)
                if slot == MID_DVE["mx2"]:
                    dve.wait_ge(mx_ready, n)
                    dve.tensor_copy(s_d[:, :], dots[:, :])
                    row_sums(s_m, sq).then_inc(mx_sums, 1)
                if slot == MID_DVE["av"]:
                    dve.wait_ge(a_ready, n)
                    dve.tensor_tensor(v[:, :, :], pt[:, :, :], per_row(co_a), ALU.mult).then_inc(av_ready, 1)
                if slot == MID_DVE["vn"]:
                    dve.wait_ge(v_squared, n)
                    row_sums(s_v, sq).then_inc(v_sum, 1)

            def final(n, slot, row):
                if slot in ("sn", FINAL_DVE["sn"]):
                    dve.wait_ge(s_ready, n)
                    row_sums(s_n, sq).then_inc(sn_ready, 1)
                if slot in ("r", FINAL_DVE["r"]):
                    dve.scalar_tensor_tensor(h0in[:, :, :], pt[:, :, :], 0.0, sq[:, :, :],
                                             ALU.is_gt, ALU.mult).then_inc(r_squared, 1)
                if slot in ("rn", FINAL_DVE["rn"]):
                    dve.wait_ge(r_squared, n)
                    row_sums(s_r, h0in).then_inc(rn_ready, 1)
                if slot in ("scale", FINAL_DVE["scale"]):
                    dve.wait_ge(f_coef, n)
                    dve.scalar_tensor_tensor(v[:, :, :], pt[:, :, :], 0.0, per_row(co_c),
                                             ALU.max, ALU.mult).then_inc(scaled, 1)

            def first_row(t, norm):
                for c in range(CH):
                    chunk(t, c)
                    if norm and c in STATS_H:
                        q = STATS_H.index(c)
                        stats_h(t + 2, range(q * HALF, (q + 1) * HALF))
            stats_h(0)
            stats_h(1)
            first_row(0, True)
            step = steps(dve, "bias")
            dve.wait_ge(const_in, 32)
            step(dve.tensor_tensor(sq[:, 0, :], hb[:, 0, :], hb[:, 0, :], ALU.mult))
            dve.tensor_reduce(s_n[:, 0:1], sq[:, 0, :], AX.X, ALU.add).then_inc(b_sum, 1)
            with dve.Fori(1, NB - 2) as t:
                first_row(t, True)
            first_row(NB - 2, False)
            step = steps(dve, "hb")
            dve.wait_ge(b_coef, 1)
            step(dve.tensor_scalar(hb[:, 0, :], hb[:, 0, :], co_c[:, 0:1], None, ALU.mult))
            step(dve.tensor_tensor(sq[:, 0, :], hb[:, 0, :], hb[:, 0, :], ALU.mult))
            dve.tensor_reduce(y2[:, 0:1], sq[:, 0, :], AX.X, ALU.add)
            step(dve.tensor_tensor(sq[:, 1, :], hb[:, 0, :], w_sb[:, :], ALU.mult))
            dve.tensor_reduce(w_hb[:, 0:1], sq[:, 1, :], AX.X, ALU.add).then_inc(b_ready, 1)
            first_row(NB - 1, False)

            with dve.Fori(*rows_after_first) as i:
                for t in range(NB):
                    for c in range(CH):
                        if t == 0 and c == SAVE:
                            save_acc(i)
                        chunk(i * NB + t, c)
                        mid(i, t * CH + c + 1)

            for t in range(NB):
                for c in range(CH):
                    if t == 0 and c == SAVE:
                        save_acc(NB)
                    chunk(P2 + t, c)
                    mid(NB, t * CH + c + 1)

            with dve.Fori(0, PAIRS) as p:
                for t in range(NB):
                    for c in range(CH):
                        if (t, c) == SAVE_BEFORE:
                            save_sum(PAIRS0 + p * NB, p, tacc)
                        if (t, c) == SAVE_SMALL:
                            wait_apart(dve, s_psum, 2 * p + 1)
                            save_sum(PAIRS0 + p * (NB + 1) + 1, NB - 1 - p, hacc)
                        chunk(PAIRS0 + p * NB + t, c)
                        finals_of_pair(p, t * CH + c + 1, final)
            for t in range(NB - LAST):
                for c in range(CH):
                    if (t, c) == SAVE_BEFORE:
                        save_sum(LAST0, LAST - 1, tacc)
                    chunk(LAST0 + t, c)
                    final(NB - 1, t * CH + c + 1, LAST - 1)
            save_sum(LAST0 + NB - LAST, LAST, hacc)
            for place in ("sn", "r", "rn"):
                final(NB, place, LAST)
            for place in ("series", "nx", "coef"):
                final_norms(dve, NB, place, LAST)
            final(NB, "scale", LAST)
            final_norms(dve, NB, "out", LAST)

        @block.gpsimd
        def _(pool):
            def stage(j, task, half, use_h, use_t):
                wait_apart(pool, whi_ready, task * 2 + half + 1)
                last = None
                if use_h:
                    last = pool.tensor_tensor(hw_lo[:, half, :], h[:, half_blk(j, half)],
                                              hw_hi[:, half, :].bitcast(F32), ALU.subtract)
                if use_t:
                    last = pool.tensor_tensor(tw_lo[:, half, :], tan[:, half_blk(j, half)],
                                              tw_hi[:, half, :].bitcast(F32), ALU.subtract)
                last.then_inc(wlo_ready, 1)

            def inverse_std(n):
                tt, ts, mul, power, norms = arithmetic(pool, "inverse_std")
                wait_apart(pool, stats_ready, n)
                step = steps(pool, "eps")
                step(pool.tensor_tensor(rstd[:, :], mv[:, :, 1], c_eps[:, :], ALU.add))
                power(rstd, rstd, c_mhalf)
                step(pool.tensor_tensor(shift[:, :], mv[:, :, 0], rstd[:, :], ALU.mult))
                ts(shift, shift, -1.0, ALU.mult, done=rstd_ready)

            def mid(n, at):
                if at == MID_POOL["pre"]:
                    step = steps(pool, "pre")
                    wait_apart(pool, rows_in, 32 * n)
                    step(pool.tensor_scalar(h0in[:, :, :], h0in[:, :, :], ALPHA, 0.0, ALU.mult, ALU.add))
                    pool.tensor_tensor(xin[:, :, :], h0in[:, :, :], xin[:, :, :], ALU.add).then_inc(pre_ready, 1)
                if at == MID_POOL["rstd"]:
                    inverse_std(NB + n)
                if at == MID_POOL["xn"]:
                    tt, ts, mul, power, norms = arithmetic(pool, "xn")
                    wait_apart(pool, xn_ready, n)
                    norms(xinv, mnorm, s_x)
                    ts(arg, mnorm, ARTANH_MAX, ALU.min, done=ln1_arg)
                if at == MID_POOL["artanh1"]:
                    ops = arithmetic(pool, "artanh1")
                    wait_apart(pool, ln1_ready, n)
                    series(ops)
                    artanh(ops, at_)
                    ops[2](xinv, at_, xinv)
                if at == MID_POOL["mxn"]:
                    tt, ts, mul, power, norms = arithmetic(pool, "mxn")
                    wait_apart(pool, mx_sums, n)
                    norms(minv, mnorm, s_m)
                    mul(arg, xinv, mnorm, done=tanh_arg)
                if at == MID_POOL["ab"]:
                    tt, ts, mul, power, norms = arithmetic(pool, "ab")
                    norm, r, xy, den = tnh, minv, T[0], T[1]
                    wait_apart(pool, tanh_ready, n)
                    ts(norm, tnh, MAX_NORM, ALU.min)
                    mul(r, norm, minv)
                    mul(norm, norm, norm)
                    step = steps(pool, "den")
                    step(pool.tensor_scalar(den[:, :], norm[:, :], y2[:, 0:1], None, ALU.mult))
                    mul(xy, r, s_d)
                    ts(xy, xy, 2.0, ALU.mult, 1.0, ALU.add)
                    tt(den, den, xy, ALU.add)
                    ts(den, den, MIN_NORM, ALU.max)
                    power(den, den, c_minus)
                    step(pool.tensor_scalar(xy[:, :], xy[:, :], y2[:, 0:1], None, ALU.add))
                    mul(xy, xy, r)
                    mul(co_a, xy, den, done=a_ready)
                    ts(norm, norm, -1.0, ALU.mult, 1.0, ALU.add)
                    mul(co_b, norm, den)
                    pool.tensor_tensor(sq[:, :, :], hb[:, :, :].to_broadcast([P, CH, F]), per_row(co_b),
                                       ALU.mult).then_inc(bhb_ready, 1)
                if at == MID_POOL["v"]:
                    wait_apart(pool, av_ready, n)
                    wait_apart(pool, bhb_ready, n)
                    pool.tensor_tensor(v[:, :, :], v[:, :, :], sq[:, :, :], ALU.add).then_inc(v_ready, 1)
                if at == MID_POOL["vn"]:
                    tt, ts, mul, power, norms = arithmetic(pool, "vn")
                    wait_apart(pool, v_sum, n)
                    norms(vinv, mnorm, s_v)
                    ts(arg, mnorm, MAX_NORM, ALU.min, done=ln2_arg)
                if at == MID_POOL["c"]:
                    ops = arithmetic(pool, "c")
                    wait_apart(pool, ln2_arg, n)
                    series(ops)
                    wait_apart(pool, ln2_ready, n)
                    artanh(ops, at_)
                    ops[2](co_c, at_, vinv)
                    tj = rows_of(tan[:, blk(n - 1)])
                    pool.tensor_tensor(tj, v[:, :, :], per_row(co_c), ALU.mult).then_inc(tan_ready, 1)

            def final(n, at, row):
                final_norms(pool, n, at, row)

            step = steps(pool, "const")
            step(pool.memset(c_mhalf[:, :], -0.5))
            step(pool.memset(c_eps[:, :], LN_EPS))
            step(pool.memset(c_minus[:, :], -1.0))
            step(pool.memset(c_one[:, :], 1.0))
            pool.memset(zeros[:, :], 0.0).then_inc(zero_ready, 1)
            pool.memset(zmove[:, :], 0.0).then_inc(zero_ready, 1)
            inverse_std(1)
            step(pool.memset(ident[:, :], 0.0))
            pool.affine_select(out=ident[:, :], in_=ident[:, :], compare_op=ALU.not_equal, fill=1.0,
                               base=0, pattern=[[-1, P]], channel_multiplier=1).then_inc(pool_const, 1)

            def first_row(t, norm):
                for half in range(2):
                    stage((3 * t + 2) % NB, t, half, True, False)
                    if norm and half == 1:
                        wait_apart(pool, h_ready, t + 2)
                        inverse_std(t + 3)
            stage(block_of(0, 0), 0, 0, True, False)
            inverse_std(2)
            stage(block_of(0, 0), 0, 1, True, False)
            wait_apart(pool, h_ready, 2)
            inverse_std(3)
            with pool.Fori(1, NB - 2) as t:
                first_row(t, True)
            first_row(NB - 2, False)
            tt, ts, mul, power, norms = arithmetic(pool, "bias", 1)
            pool.wait_ge(b_sum, 1)
            norms(xinv, arg, s_n, norm_done=b_arg)
            pool.wait_ge(b_tanh, 1)
            ts(co_a, tnh, MAX_NORM, ALU.min)
            mul(co_c, co_a, xinv, done=b_coef)
            first_row(NB - 1, False)
            pool.wait_ge(b_ready, 1)

            with pool.Fori(*rows_after_first) as i:
                for t in range(NB):
                    j, task = pool.snap(block_of(i, t)), i * NB + t

                    def halves(use_t):
                        for half in range(2):
                            stage(j, task, half, True, use_t)
                            mid(i, 2 * t + half)
                    if t == NB - 1:
                        halves(True)
                    else:
                        with pool.If(j < i):
                            halves(True)
                        with pool.Else():
                            halves(False)
            for t in range(NB):
                for half in range(2):
                    stage(t, P2 + t, half, False, True)
                    mid(NB, 2 * t + half)

            with pool.Fori(0, PAIRS) as p:
                for t in range(NB):
                    def halves(j):
                        for half in range(2):
                            stage(j, PAIRS0 + p * NB + t, half, False, True)
                            at = 2 * t + half
                            if at < NB:
                                final(2 * p + 1, at, p)
                            else:
                                final(2 * p + 2, at - NB, NB - 1 - p)
                    if t == 0:
                        halves(NB - 1 - p)
                    elif t < PAIRS:
                        with pool.If(p >= t):
                            halves(small_row_block(p, t))
                        with pool.Else():
                            halves(t)
                    else:
                        halves(t)
            for t in range(NB - LAST):
                for half in range(2):
                    stage(LAST + t, LAST0 + t, half, False, True)
                    final(NB - 1, 2 * t + half, LAST - 1)
            final(NB, "sn", LAST)

        @block.tensor
        def _(pe):
            def product(acc, w_hi, w_lo, half, c, start):
                slot, w = c % SPLITS, bass.ts(c % HALF, F)
                last = None
                for n, (ws, a) in enumerate(((w_hi, a_hi), (w_lo, a_hi), (w_hi, a_lo))):
                    for b in range(BANKS):
                        last = pe.matmul(acc[:, bass.ts(b, BANK)], ws[:, half, w], a[:, slot, bass.ts(b, BANK)],
                                         start=start and n == 0, stop=False, skip_group_check=True)
                return last

            def chunk(task, c, use_h, use_t, start_h=False, acc=tacc, start=False, row=None):
                if c % HALF == 0:
                    pe.wait_ge(wlo_ready, task * 2 + c // HALF + 1)
                pe.wait_ge(lo_ready, task * CH + c + 1)
                last = None
                if use_h:
                    last = product(hacc, hw_hi, hw_lo, c // HALF, c, start_h and c == 0)
                if row is not None:
                    pe.wait_ge(acc_saved, 2 * row)
                    zero_tacc()
                if use_t:
                    last = product(acc, tw_hi, tw_lo, c // HALF, c, start and c == 0)
                last.then_inc(chunk_used, 1)

            def zero_tacc():
                for b in range(BANKS):
                    pe.matmul(tacc[:, bass.ts(b, BANK)], zeros[:, :], zmove[:, :], start=True, stop=False,
                              skip_group_check=True)

            def transpose(src, signal):
                last = None
                for c in range(CH):
                    last = pe.transpose(pt[:, c, :], src(c), ident[:, :])
                last.then_inc(signal, 1)

            def mid(n, slot):
                if slot == MID_PE["y"]:
                    transpose(lambda c: accT[:, bass.ts(c, P)], y_psum)
                if slot == MID_PE["h2T"]:
                    pe.wait_ge(h2_ready, n)
                    transpose(lambda c: z[:, c, :], h2t_psum)
                if slot == MID_PE["mx"]:
                    pe.wait_ge(h2t_ready, n)
                    last = None
                    for c in range(CH):
                        pe.matmul(pt[:, c, :], accT[:, bass.ts(c, P)], w_sb[:, :], start=True, stop=True)
                        last = pe.matmul(dots[:, c:c + 1], accT[:, bass.ts(c, P)], w_hb[:, :], start=True, stop=True)
                    last.then_inc(mx_psum, 1)

            def final(n, slot, row):
                if slot in ("s", FINAL_PE["s"]):
                    wait_apart(pe, acc_saved, 2 * NB + n)
                    transpose(lambda c: accT[:, bass.ts(c, P)], s_psum)

            pe.wait_ge(zero_ready, 2)
            pe.wait_ge(pool_const, 1)
            zero_tacc()
            for c in range(CH):
                chunk(0, c, True, False, start_h=True)
            pe.wait_ge(const_in, 32)
            with pe.Fori(1, NB) as t:
                for c in range(CH):
                    chunk(t, c, True, False)

            with pe.Fori(*rows_after_first) as i:
                pe.wait_ge(hacc_saved, 2 * i)
                for t in range(NB):
                    j, task = pe.snap(block_of(i, t)), i * NB + t

                    def chunks(use_t):
                        for c in range(CH):
                            chunk(task, c, True, use_t, start_h=t == 0, row=i if (t, c) == (0, 0) else None)
                            mid(i, t * CH + c + 1)
                    if t == NB - 1:
                        chunks(True)
                    else:
                        with pe.If(j < i):
                            chunks(True)
                        with pe.Else():
                            chunks(False)
            pe.wait_ge(acc_saved, 2 * NB)
            zero_tacc()
            for t in range(NB):
                for c in range(CH):
                    chunk(P2 + t, c, False, True)
                    mid(NB, t * CH + c + 1)

            with pe.Fori(0, PAIRS) as p:
                for t in range(NB):
                    def chunks(acc):
                        if t == 0:
                            wait_apart(pe, acc_saved, 2 * NB + 2 * p)
                        for c in range(CH):
                            chunk(PAIRS0 + p * NB + t, c, False, True, acc=acc, start=t == 0)
                            finals_of_pair(p, t * CH + c + 1, final)
                        if t == 0:
                            wait_apart(pe, acc_saved, 2 * NB + 2 * p + 1)
                            zero_tacc()
                    if t == 0:
                        chunks(hacc)
                    elif t < PAIRS:
                        with pe.If(p >= t):
                            chunks(hacc)
                        with pe.Else():
                            chunks(tacc)
                    else:
                        chunks(tacc)
            pe.wait_ge(acc_saved, 2 * NB + 2 * PAIRS)
            for t in range(NB - LAST):
                for c in range(CH):
                    chunk(LAST0 + t, c, False, True, acc=hacc, start=t == 0)
                    final(NB - 1, t * CH + c + 1, LAST - 1)
            pe.wait_ge(acc_saved, 2 * NB + 2 * PAIRS + 2)
            final(NB, "s", LAST)


def kernel(x, adj, L0_gnn_h, L1_gnn_weight, L1_gnn_bias):
    import concourse.bacc as bacc
    from concourse.bass_utils import run_bass_kernel_spmd

    def rows(a):
        return np.ascontiguousarray(a).reshape(NB, P, CH * F)

    blocks = np.asarray(adj).reshape(NB, P, CH, NB, P, LOADS, PER_LOAD).transpose(0, 3, 5, 4, 6, 2, 1)
    arrays = {
        "x": rows(x),
        "adj": np.ascontiguousarray(blocks).reshape(NB, NB, LOADS, P, PER_LOAD * BLK),
        "h0": rows(L0_gnn_h),
        "wt": np.ascontiguousarray(np.asarray(L1_gnn_weight).T),
        "bias": np.ascontiguousarray(L1_gnn_bias).reshape(1, F),
    }
    nc = bacc.Bacc("TRN2", target_bir_lowering=False, num_devices=1)
    args = [nc.dram_tensor(n, a.shape, F32, kind="ExternalInput").ap() for n, a in arrays.items()]
    out = nc.dram_tensor("out", (NB, P, CH * F), F32, kind="ExternalOutput").ap()
    build(nc, *args, out)
    r = run_bass_kernel_spmd(nc, [arrays], core_ids=[0])
    return r.results[0]["out"].reshape(N, F)
```
